# Optimizing a Trainium2 kernel written in Bass

```python
import numpy as np
import jax
import jax.numpy as jnp

def _softmax(x, axis=-1):
    return jax.nn.softmax(x, axis=axis)

def _gelu(x):
    return jax.nn.gelu(x, approximate=True)

def _silu(x):
    return jax.nn.silu(x)

def _sigmoid(x):
    return jax.nn.sigmoid(x)

def _layernorm(x, axis=-1, eps=1e-05):
    m = jnp.mean(x, axis=axis, keepdims=True)
    v = jnp.var(x, axis=axis, keepdims=True)
    return (x - m) / jnp.sqrt(v + eps)

def _scatter_add(tgt, idx, src, axis=0):
    return tgt.at[idx].add(src)

def _segment_sum(src, seg, n):
    return jax.ops.segment_sum(src, seg, n)
kernel_name = 'mk_macaron_d1_jaxref_r8_7b21a2'

def setup_inputs(seed: int=0):
    np.random.seed(seed)
    _w = jnp.asarray

    def _L0_attn_setup():
        import jax, jax.numpy as jnp
        import numpy as np
        HIDDEN = 256
        N_HEADS = 16
        N_KV_HEADS = 4
        HEAD_DIM = 128
        THETA = 10000.0
        MASK_NEG = -2.3819763e+38

        def apply_rotary_emb(x, theta=THETA):
            B, S, H, D = x.shape
            half = D // 2
            freqs = 1.0 / theta ** (jnp.arange(0, D, 2, dtype=jnp.float32) / D)
            ang = jnp.arange(S, dtype=jnp.float32)[:, None] * freqs[None, :]
            cos = jnp.cos(ang)[None, :, None, :]
            sin = jnp.sin(ang)[None, :, None, :]
            xf = x.astype(jnp.float32)
            x1, x2 = (xf[..., :half], xf[..., half:])
            real = x1 * cos - x2 * sin
            imag = x1 * sin + x2 * cos
            return jnp.concatenate([real, imag], axis=-1).astype(x.dtype)
        key = jax.random.key(seed)
        k1, k2, k3 = jax.random.split(key, 3)
        B, S = (2, 256)
        lim_qkv = 1.0 / np.sqrt(HIDDEN)
        lim_o = 1.0 / np.sqrt(N_HEADS * HEAD_DIM)
        x = jax.random.normal(k1, (B, S, HIDDEN), dtype=jnp.float32)
        Wqkv = jax.random.uniform(k2, (HIDDEN, (N_HEADS + 2 * N_KV_HEADS) * HEAD_DIM), minval=-lim_qkv, maxval=lim_qkv, dtype=jnp.float32)
        Wo = jax.random.uniform(k3, (N_HEADS * HEAD_DIM, HIDDEN), minval=-lim_o, maxval=lim_o, dtype=jnp.float32)
        return {'x': x, 'Wqkv': Wqkv, 'Wo': Wo}
    _L0_attn_in = _L0_attn_setup()

    def _L0_ffn_setup():
        import jax, jax.numpy as jnp
        import numpy as np
        B, T, D, F, E, K = (2, 128, 256, 96, 16, 2)
        key = jax.random.key(seed)
        k0, k1, k2, k3, k4 = jax.random.split(key, 5)
        scale = 0.02
        return {'x': jax.random.normal(k0, (B, T, D), dtype=jnp.float32), 'router_w': jax.random.normal(k1, (D, E), dtype=jnp.float32) * scale, 'gate_w': jax.random.normal(k2, (E, D, F), dtype=jnp.float32) * scale, 'up_w': jax.random.normal(k3, (E, D, F), dtype=jnp.float32) * scale, 'down_w': jax.random.normal(k4, (E, F, D), dtype=jnp.float32) * scale}
    _L0_ffn_in = _L0_ffn_setup()
    _d = {'L0_attn_x': _L0_attn_in['x'], 'L0_attn_Wqkv': _L0_attn_in['Wqkv'], 'L0_attn_Wo': _L0_attn_in['Wo'], 'L0_ffn_router_w': _L0_ffn_in['router_w'], 'L0_ffn_gate_w': _L0_ffn_in['gate_w'], 'L0_ffn_up_w': _L0_ffn_in['up_w'], 'L0_ffn_down_w': _L0_ffn_in['down_w']}
    _x0 = _d['L0_attn_x']
    _d['L0_attn_x'] = jax.random.normal(jax.random.fold_in(jax.random.key(seed), 1), (4, 512, 256), dtype=_x0.dtype)
    del _x0
    return _d

def reference(L0_attn_x, L0_attn_Wqkv, L0_attn_Wo, L0_ffn_router_w, L0_ffn_gate_w, L0_ffn_up_w, L0_ffn_down_w):

    def _L0_attn_ref(x, Wqkv, Wo):
        import jax, jax.numpy as jnp
        import numpy as np
        HIDDEN = 256
        N_HEADS = 16
        N_KV_HEADS = 4
        HEAD_DIM = 128
        THETA = 10000.0
        MASK_NEG = -2.3819763e+38

        def apply_rotary_emb(x, theta=THETA):
            B, S, H, D = x.shape
            half = D // 2
            freqs = 1.0 / theta ** (jnp.arange(0, D, 2, dtype=jnp.float32) / D)
            ang = jnp.arange(S, dtype=jnp.float32)[:, None] * freqs[None, :]
            cos = jnp.cos(ang)[None, :, None, :]
            sin = jnp.sin(ang)[None, :, None, :]
            xf = x.astype(jnp.float32)
            x1, x2 = (xf[..., :half], xf[..., half:])
            real = x1 * cos - x2 * sin
            imag = x1 * sin + x2 * cos
            return jnp.concatenate([real, imag], axis=-1).astype(x.dtype)
        B, S, _ = x.shape
        q_size = N_HEADS * HEAD_DIM
        kv_size = N_KV_HEADS * HEAD_DIM
        g = N_HEADS // N_KV_HEADS
        xqkv = x @ Wqkv
        xq = xqkv[..., :q_size].reshape(B, S, N_HEADS, HEAD_DIM)
        xk = xqkv[..., q_size:q_size + kv_size].reshape(B, S, N_KV_HEADS, HEAD_DIM)
        xv = xqkv[..., q_size + kv_size:].reshape(B, S, N_KV_HEADS, HEAD_DIM)
        xq = apply_rotary_emb(xq)
        xk = apply_rotary_emb(xk)
        xk = jnp.repeat(xk, g, axis=2)
        xv = jnp.repeat(xv, g, axis=2)
        scale = HEAD_DIM ** (-0.5)
        scores = jnp.einsum('bqhd,bkhd->bhqk', xq, xk) * scale
        causal_add = jnp.triu(jnp.full((S, S), MASK_NEG, dtype=jnp.float32), k=1)
        scores = scores + causal_add[None, None]
        probs = jax.nn.softmax(scores, axis=-1)
        attn = jnp.einsum('bhqk,bkhd->bqhd', probs, xv).reshape(B, S, q_size)
        return attn @ Wo

    def _L0_ffn_ref(x, router_w, gate_w, up_w, down_w):
        import jax, jax.numpy as jnp
        import numpy as np
        B, T, D, F, E, K = (2, 128, 256, 96, 16, 2)
        scores = jnp.einsum('btd,de->bte', x, router_w).astype(jnp.float32)
        probs = jax.nn.softmax(scores, axis=-1)
        routing_weights, routing_idx = jax.lax.top_k(probs, K)
        routing_weights = routing_weights / jnp.sum(routing_weights, axis=-1, keepdims=True)
        routing_weights = routing_weights.astype(x.dtype)
        one_hot = jax.nn.one_hot(routing_idx, E, dtype=x.dtype)
        combine = jnp.einsum('btk,btke->bte', routing_weights, one_hot)
        g = jnp.einsum('btd,edf->ebtf', x, gate_w)
        u = jnp.einsum('btd,edf->ebtf', x, up_w)
        h = jax.nn.silu(g) * u
        expert_out = jnp.einsum('ebtf,efd->ebtd', h, down_w)
        out = jnp.einsum('ebtd,bte->btd', expert_out, combine)
        return out
    x = L0_attn_x
    x = x + 0.5 * _L0_ffn_ref(_layernorm(x, axis=-1), L0_ffn_router_w, L0_ffn_gate_w, L0_ffn_up_w, L0_ffn_down_w)
    x = x + _L0_attn_ref(_layernorm(x, axis=-1), L0_attn_Wqkv, L0_attn_Wo)
    x = x + 0.5 * _L0_ffn_ref(_layernorm(x, axis=-1), L0_ffn_router_w, L0_ffn_gate_w, L0_ffn_up_w, L0_ffn_down_w)
    return x

_drawn_inputs = setup_inputs


def setup_inputs(seed=0):
    import zlib

    import numpy as np

    out = dict(_drawn_inputs(seed))
    spreads = {}
    factors = {'L0_ffn_router_w': 8.0,
     'L0_ffn_gate_w': 7.789,
     'L0_ffn_up_w': 7.719,
     'L0_ffn_down_w': 7.69}
    for name, (base, spread) in spreads.items():
        noise = np.random.default_rng([zlib.crc32(name.encode()), seed]).standard_normal(out[name].shape)
        drawn = base * np.exp(spread * noise) if base else spread * noise
        out[name] = jnp.asarray(drawn.astype(out[name].dtype))
    for name, factor in factors.items():
        out[name] = (out[name] * factor).astype(out[name].dtype)
    return out
```

```python
from contextlib import ExitStack

import concourse.bass as bass
import numpy as np
from concourse import mybir

F32 = mybir.dt.float32
F32R = mybir.dt.float32r
BF16 = mybir.dt.bfloat16
I32 = mybir.dt.int32
ALU = mybir.AluOpType
ACT = mybir.ActivationFunctionType
AX_X = mybir.AxisListType.X

P = 128
EPS = 1e-5


class Sizes:

    def __init__(self, x, wqkv, wo, router, gate):
        self.B, self.S, self.D = x
        self.E, _, self.F = gate
        self.EF = self.E * self.F
        self.NC = self.EF // P
        self.T = self.S // P
        self.K = self.D // P
        self.H = wo[0] // P
        self.KV = (wqkv[1] // P - self.H) // 2
        self.G = self.H // self.KV
        self.UG = self.NC
        self.UD = self.NC // 2
        self.UF = self.UG + self.UD
        self.UQ = self.KV * 3
        self.UO = self.H // 2
        self.UA = self.UQ + self.UO


def build(nc, A, z, attn=True, ffn2=True):
    with ExitStack() as ctx:
        program(nc, A, z, ctx, attn, ffn2)


def program(nc, A, z, ctx, attn, ffn2):
    B, S, D, E, T, K, NC, G, KV = z.B, z.S, z.D, z.E, z.T, z.K, z.NC, z.G, z.KV

    def sb(name, shape, dt, at=ctx):
        return at.enter_context(nc.sbuf_tensor("sb_" + name, shape, dt))

    def sem(name):
        return ctx.enter_context(nc.semaphore(name))

    wF = sb("wF", [P, 2 * z.UF, 512], F32R)
    wA = sb("wA", [P, 2 * z.UA, 512], F32R)
    x = sb("x", [P, B, T, D], F32)
    xf = sb("xf", [P, K, S], F32)
    xh = sb("xh", [P, K, S], F32R)
    xl = sb("xl", [P, K, S], F32R)
    work = sb("work", [P, T * D], F32)
    ident = sb("ident", [P, P], F32)
    identb = sb("identb", [P, P], BF16)
    causal = sb("causal", [P, P], BF16)
    router = sb("router", [P, K, E], F32)
    revidx = sb("revidx", [P, E], F32)
    stats = sb("stats", [P, T, 6], F32)
    mv = sb("mv", [P, 5, T], F32)
    rs = sb("rs", [P, 4, T], F32)
    nmax = sb("nmax", [P, 2, G], F32)
    ssum = sb("ssum", [P, 2, G], F32)
    rinv = sb("rinv", [P, 2, G], F32)

    with ExitStack() as own:
        stage = sb("stage", [P, 4, 512], F32, own)
        hh = sb("hh", [P, 2, 512], F32R, own)
        hl = sb("hl", [P, 2, 512], F32R, own)
        expand = sb("expand", [P, z.EF], BF16, own)
        combT = sb("combT", [P, S], BF16, own)
        comb = sb("comb", [P, T, P], BF16, own)
        lg = sb("lg", [P, 5, T, E], F32, own)
        lm = sb("lm", [P, 4, T], F32, own)
    if attn:
        own = ctx.enter_context(ExitStack())
        prob = [sb("prob0", [P, G, S - P], F32, own), sb("prob1", [P, G, S], F32, own)]
        ropeA = sb("ropeA", [P, S], F32, own)
        ropeB = sb("ropeB", [P, S], F32, own)
        cos = sb("cos", [P, S], F32, own)
        sin = sb("sin", [P, S], F32, own)

    ps = ctx.enter_context(nc.psum_tensor("ps", [P, 8, 512], F32))
    GATE, UP, CB, DOWN, MISC, LOG = 0, 1, 2, 3, 5, 7

    raw_in = [sem(f"raw_in{i}") for i in range(4)]
    w_hi = sem("w_hi")
    w_lo_d = sem("w_lo_d")
    w_lo_p = sem("w_lo_p")
    x_in = sem("x_in")
    const_in = sem("const_in")
    gate_done = sem("gate_done")
    up_done = sem("up_done")
    cb_done = sem("cb_done")
    down_done = sem("down_done")
    silu_done = sem("silu_done")
    su_done = sem("su_done")
    h_done = sem("h_done")
    hi_done = sem("hi_done")
    lo_done = sem("lo_done")
    stat_step = sem("stat_step")
    xn_done = sem("xn_done")
    xnT_done = sem("xnT_done")
    xf_done = sem("xf_done")
    xh_done = sem("xh_done")
    xl_done = sem("xl_done")
    logit_done = sem("logit_done")
    lshift_done = sem("lshift_done")
    lexp_done = sem("lexp_done")
    comb_done = sem("comb_done")
    combT_ps = sem("combT_ps")
    combT_done = sem("combT_done")
    ffn_evac = sem("ffn_evac")
    ffn_back = sem("ffn_back")
    x_done = sem("x_done")
    out_done = sem("out_done")
    comb_zero = sem("comb_zero")

    sems = """aw_lo aw_hi tab_in ax_hi ax_lo axn_done axT_done axf_done proj_done proj_act proj_dve rope_mul rope_sum
        q_hi q_lo s_done nmax_done exp_done norm_done recip_done pt_done pt_hi pt_lo pv_done a_hi a_lo wo_done xadd_done v_hi v_lo refill""".split()
    sm = {n: sem(n) for n in sems}
    aw_in = [sem(f"aw_in{i}") for i in range(2)]
    (aw_lo, aw_hi, tab_in, ax_hi, ax_lo, axn_done, axT_done, axf_done, proj_done, proj_act, proj_dve, rope_mul, rope_sum,
     q_hi, q_lo, s_done, nmax_done, exp_done, norm_done, recip_done, pt_done, pt_hi, pt_lo, pv_done, a_hi, a_lo, wo_done,
     xadd_done, v_hi, v_lo, refill) = (sm[n] for n in sems)

    UB = KV * T
    PB = KV * T * (T + 1) // 2
    SBANK, TBANK, OBANK, WBANK, JBANK = 0, 3, 5, 6, 7

    def tiles_before(k):
        g, i = divmod(k, T)
        return g * T * (T + 1) // 2 + i * (i + 1) // 2

    def bank_of(m):
        return SBANK + (1 if m == UB * G - 1 else m % 3)

    def bank_before(m):
        M = UB * G
        return next(d for d in range(1, 9) if bank_of((m - d) % M) == bank_of(m % M))

    KCOL, VCOL = G, G + 1
    TASKS = {0: [("mid", KCOL)], 1: [("mid", 0)], 2: [("mid", 1), ("end", 2)], 3: [("mid", 3), ("end", VCOL)]}
    LN_AT = 11
    order = [(k, place, col) for k in range(UB) for place in ("mid", "end") for pl, col in
             ([(p_, c_) for p_, c_ in TASKS[k % T] if p_ == place] + ([("end", -1 - kk) for kk in range(K)] if k == LN_AT and place == "end" else []))]
    JN = len(order)

    def task_count(k, place, col):
        more, k = divmod(k, UB)
        n = order.index((k, place, col))
        before = order[:n]
        dv = sum(c >= 0 for _, _, c in before)
        vs = sum(c == VCOL for _, _, c in before)
        full_dv, full_vs = sum(c >= 0 for _, _, c in order), KV
        first = (K + G + 2, G + 2, 1)
        return (first[0] + more * JN + n, first[1] + more * full_dv + dv,
                first[1] - 1 + more * (full_dv - full_vs) + dv - vs, first[2] + more * full_vs + vs)

    JB = JN, (G + 2) * KV, (G + 1) * KV, KV

    def set_base(g):
        return 24 if g % 2 == 0 else 0

    def q_at(g, h, part):
        return wF[:, set_base(g) + 2 * h + part]

    def k_at(g, part):
        return wF[:, set_base(g) + 2 * G + part]

    def v_at(g, part):
        return wF[:, set_base(g) + 2 * G + 2 + part]

    def pT_at(n, part):
        return wF[:, 12 + 2 * (n % 4) + part]

    def a_at(k, part):
        return wF[:, 20 + 2 * (k % 2) + part]

    def qkv_w(g, col, k, part):
        at = (col % 2) * D + k * P
        return wA[:, 2 * (3 * g + col // 2) + part, at:at + P]

    def wo_w(g, h, part):
        hq = G * g + h
        at = (hq % 2) * D
        return wA[:, 2 * (z.UQ + hq // 2) + part, at:at + D]

    SCALE = float(P) ** -0.5
    HP = P // 2

    AU = z.UA // B
    FIRST = [KCOL, *range(G), VCOL]
    PEEL = 3
    LAST_GROUP = UB - T

    def tasks_at(k, which):
        return [(place, col) for kk, place, col in order
                if kk == k % UB and which and (which is True or (kk < LAST_GROUP and col >= 0))]

    def run_steps(eng, step):
        for k in range(PEEL):
            step(0, k, True, k > 0, True)
        with eng.Fori(0, B - 1) as b:
            for k in range(PEEL, UB + PEEL):
                step(b, k, True, True, True)
        for k in range(PEEL, UB):
            step(B - 1, k, True, True, "own")
        step(B - 1, UB, False, True, False)
        step(B - 1, UB + 1, False, False, False)

    def ffn_w(turn, u, part):
        return wF[:, 2 * u + part] if turn == 0 or u >= z.UG else wA[:, 2 * u + part]

    def gu_w(wt, c, which, k, part):
        at = (2 * which + k) * P
        return wt[:, 2 * c + part, at:at + P]

    def down_w(wt, base, c, k, part):
        at = (c % 2) * D + k * P
        return wt[:, 2 * (base + c // 2) + part, at:at + P]

    chain = {"n": 0, "loop": 0}

    block = ctx.enter_context(nc.Block())

    N1 = B

    @block.sync
    def _(sp):
        for b in range(B):
            if b == 1:
                sp.dma_start(ident[:], A["ident"]).then_inc(const_in, 16)
                sp.dma_start(router[:], A["router"]).then_inc(const_in, 16)
                sp.dma_start(revidx[:], A["revidx"]).then_inc(const_in, 16)
                sp.dma_start(identb[:], A["identb"]).then_inc(const_in, 16)
                sp.dma_start(expand[:], A["expand"]).then_inc(const_in, 16)
                sp.dma_start(causal[:], A["causal"]).then_inc(const_in, 16)
            sp.dma_start(x[:, b], A["x"][b]).then_inc(x_in, 16)
            if b == 0:
                for u in range(4):
                    sp.dma_start(stage[:, u], A["wffn"][u]).then_inc(raw_in[u], 16)
        for u in range(4, z.UF):
            sp.wait_ge(w_lo_p if u % 2 else w_lo_d, (u - 4) // 2 + 1)
            sp.dma_start(stage[:, u % 4], A["wffn"][u]).then_inc(raw_in[u % 4], 16)
        if attn:
            sp.wait_ge(w_lo_d, z.UF // 2)
            sp.wait_ge(w_lo_p, z.UF // 2)
            for j in range(AU):
                if j >= 2:
                    sp.wait_ge(aw_lo, j - 1)
                sp.dma_start(stage[:, j % 2], A["wattn"][j]).then_inc(aw_in[j % 2], 16)
            with sp.Fori(1, B) as b:
                for j in range(AU):
                    sp.wait_ge(aw_lo, b * AU + max(j - 1, 0))
                    sp.dma_start(stage[:, j % 2], A["wattn"][bass.ds(b * AU + j, 1)].rearrange("a p c -> p (a c)"))\
                      .then_inc(aw_in[j % 2], 16)
            sp.wait_ge(down_done, B * NC)
            sp.wait_ge(lo_done, B * NC)
            sp.dma_start(cos[:], A["cos"]).then_inc(tab_in, 16)
            sp.dma_start(sin[:], A["sin"]).then_inc(tab_in, 16)
        if ffn2:
            sp.wait_ge(xadd_done, B * UB)
            sp.dma_start(expand[:], A["expand"]).then_inc(refill, 16)
            for u in range(z.UF):
                if u >= 4:
                    sp.wait_ge(w_lo_p if u % 2 else w_lo_d, z.UF // 2 + (u - 4) // 2 + 1)
                sp.dma_start(stage[:, u % 4], A["wffn"][u]).then_inc(raw_in[u % 4], 16)
            for b in range(B):
                sp.wait_ge(x_done, N1 + b + 1)
                sp.dma_start(A["out"][b], x[:, b]).then_inc(out_done, 16)
        else:
            for b in range(B):
                sp.wait_ge(xadd_done, B * UB) if attn else sp.wait_ge(x_done, b + 1)
                sp.dma_start(A["out"][b], x[:, b]).then_inc(out_done, 16)
        sp.wait_ge(out_done, 16 * B)

    @block.scalar
    def _(act):
        def weights_hi(turn, u):
            act.wait_ge(raw_in[u % 4], 16 * (u // 4 + 1 + turn * len(range(u % 4, z.UF, 4))))
            nc.scalar.activation(ffn_w(turn, u, 0), stage[:, u % 4], ACT.Copy).then_inc(w_hi, 1)

        def attn_w_hi(b, j):
            act.wait_ge(aw_in[j % 2], 16 * (len(range(j % 2, AU, 2)) * b + j // 2 + 1))
            dst = wA[:, 2 * (AU * b + j)] if type(b) is int else \
                wA[:, bass.ds((b * AU + j) * 2, 1)].rearrange("p a c -> p (a c)")
            nc.scalar.activation(dst, stage[:, j % 2], ACT.Copy).then_inc(aw_hi, 1)

        def xf_copy(n):
            act.wait_ge(xnT_done, n + 1)
            nc.scalar.activation(xf[:], ps[:, MISC:MISC + 2], ACT.Copy).then_inc(xf_done, 1)

        def x_hi(n):
            for k in range(K):
                nc.scalar.activation(xh[:, k], xf[:, k], ACT.Copy).then_inc(xh_done, 1)

        def logit_exp(n):
            act.wait_ge(lshift_done, n + 1)
            nc.scalar.activation(lg[:, 1], lg[:, 0], ACT.Exp).then_inc(lexp_done, 1)

        def combT_copy(n):
            act.wait_ge(combT_ps, n + 1)
            nc.scalar.activation(combT[:], ps[:, LOG].bitcast(BF16)[:, 0:S], ACT.Copy).then_inc(combT_done, 1)

        def silu(n, c):
            cc = n * NC + c
            act.wait_ge(gate_done, cc + 1)
            if not (type(n) is int and cc < 2):
                act.wait_ge(lo_done, n * NC + (c - 1 if c != 1 else 1))
            nc.scalar.activation(stage[:, 2 + c % 2], ps[:, GATE], ACT.Silu).then_inc(silu_done, 1)

        def h_hi(n, c):
            cc = n * NC + c
            act.wait_ge(h_done, cc + 1)
            if not (type(n) is int and cc < 2):
                act.wait_ge(down_done, n * NC + (c - 1 if c != 1 else 1))
            nc.scalar.activation(hh[:, c % 2], stage[:, 2 + c % 2], ACT.Copy).then_inc(hi_done, 1)

        def first(n):
            xf_copy(n)
            act.wait_ge(xf_done, n + 1)
            x_hi(n)
            logit_exp(n)
            combT_copy(n)

        def batch(turn, n, last):
            for c in range(1, NC + 1):
                if c < NC or not last:
                    if c == NC:
                        act.wait_ge(up_done, (n + 1) * NC)
                        act.wait_ge(xf_done, n + 2)
                        x_hi(n + 1)
                        act.wait_ge(cb_done, (n + 1) * NC)
                        combT_copy(n + 1)
                    silu(n, c) if c < NC else silu(n + 1, 0)
                    h_hi(n, c) if c < NC else h_hi(n + 1, 0)
                if turn == 0 and attn and c % 2 and c // 2 < AU:
                    attn_w_hi(n, c // 2)
                if c == 4 and not last:
                    act.wait_ge(logit_done, n + 1)
                    act.wait_ge(xl_done, n + 1)
                    xf_copy(n + 1)
                if c == 7 and not last:
                    logit_exp(n + 1)
            act.wait_ge(down_done, (n + 1) * NC)
            nc.scalar.activation(work[:], ps[:, DOWN:DOWN + 2], ACT.Copy, scale=0.5).then_inc(ffn_evac, 1)

        def ffn(n0):
            first(n0)
            silu(n0, 0)
            h_hi(n0, 0)
            with act.Fori(n0, n0 + B - 1) as n:
                batch(n0 // B, n, False)
            batch(n0 // B, n0 + B - 1, True)

        def ax_copy(b, kk, n):
            act.wait_ge(proj_done, n + 1)
            if not (type(b) is int and b < 0):
                act.wait_ge(ax_lo, K * (b + 1))
            nc.scalar.activation(xf[:, kk], ps[:, JBANK], ACT.Copy).then_inc(proj_act, 1)

        def ax_his(b):
            for kk in range(K):
                nc.scalar.activation(xh[:, kk], xf[:, kk], ACT.Copy).then_inc(ax_hi, 1)

        def task(b, k, place, col, counts=None):
            c = counts or [JB[i] * b + v for i, v in enumerate(task_count(k, place, col))]
            if col < 0:
                return ax_copy(b, -1 - col, c[0])
            g = k // T + 1
            act.wait_ge(proj_done, c[0] + 1)
            if col == VCOL:
                if k >= 0:
                    act.wait_ge(pv_done, b * PB + max(tiles_before(g * T - T), 1))
                nc.scalar.activation(v_at(g, 0), ps[:, JBANK], ACT.Copy).then_inc(proj_act, 1)
                return
            act.wait_ge(q_lo, c[2])
            act.wait_ge(proj_dve, c[1] + 1)
            scale = 1.0 if col == KCOL else SCALE
            nc.scalar.activation(ropeB[0:HP], ps[HP:P, JBANK], ACT.Copy, scale=scale)
            nc.scalar.activation(ropeB[HP:P], ps[0:HP, JBANK], ACT.Copy, scale=scale).then_inc(proj_act, 1)

        def rope_hi(b, k, place, col, counts=None):
            c = counts or [JB[i] * b + v for i, v in enumerate(task_count(k, place, col))]
            g = k // T + 1
            act.wait_ge(rope_sum, c[2] + 1)
            if k >= 0:
                act.wait_ge(s_done, b * UB * G + max((g - 1) * T * G, 1))
            dst = k_at(g, 0) if col == KCOL else q_at(g, col, 0)
            nc.scalar.activation(dst, ropeA[:], ACT.Copy).then_inc(q_hi, 1)

        def exp(b, k, h):
            i = k % T
            m = b * UB * G + k * G + h
            act.wait_ge(nmax_done, m + 1)
            if not (type(b) is int and b == 0 and k < 2):
                act.wait_ge(pt_done, b * PB + tiles_before(k - 1))
            nc.scalar.activation(prob[k % 2][:, h, 0:(i + 1) * P], ps[:, bank_of((k * G + h) % (UB * G)), 0:(i + 1) * P],
                                 ACT.Exp, bias=nmax[:, k % 2, h:h + 1], accum_out=ssum[:, k % 2, h:h + 1]).then_inc(exp_done, 1)

        def pt_his(b, k, j):
            n = b * PB + tiles_before(k) + j
            act.wait_ge(pt_done, n + 1)
            if not (type(b) is int and b == 0 and tiles_before(k) + j < 4):
                act.wait_ge(pv_done, b * PB + max(tiles_before(k) + j - 3, 1))
            nc.scalar.activation(pT_at(tiles_before(k) + j, 0), ps[:, TBANK + (tiles_before(k) + j) % 2], ACT.Copy).then_inc(pt_hi, 1)

        def a_his(b, k):
            act.wait_ge(pv_done, b * PB + tiles_before(k + 1))
            if not (type(b) is int and b == 0 and k < 2):
                act.wait_ge(wo_done, b * UB + k - 1)
            nc.scalar.activation(a_at(k, 0), ps[:, OBANK], ACT.Copy).then_inc(a_hi, 1)

        def step(b, k, scores, values, tasks):
            i, ip = k % T, (k - 1) % T
            jobs = tasks_at(k, tasks)
            if k % UB == LAST_GROUP and tasks is True:
                act.wait_ge(proj_done, JN * (b + k // UB) + task_count(LAST_GROUP - 1, "end", VCOL)[0] + 1)
                act.wait_ge(proj_act, JN * (b + k // UB) + task_count(LN_AT, "end", -K)[0] + 1)
                ax_his(b)
            for h in range(G):
                if scores:
                    exp(b, k, h)
                if h >= 1 and values and h - 1 <= ip:
                    pt_his(b, k - 1, h - 1)
                if h == 1:
                    for place, col in jobs:
                        if place == "mid":
                            task(b, k, place, col)
            if values and ip >= G - 1:
                pt_his(b, k - 1, G - 1)
            for place, col in jobs:
                if place == "mid":
                    rope_hi(b, k, place, col)
            if values:
                a_his(b, k - 1)
            for place, col in jobs:
                if place == "end":
                    task(b, k, place, col)
            for place, col in jobs:
                if place == "end" and 0 <= col < VCOL:
                    rope_hi(b, k, place, col)

        def attention():
            act.wait_ge(down_done, B * NC)
            act.wait_ge(lo_done, B * NC)
            for kk in range(K):
                ax_copy(-1, kk, kk)
            act.wait_ge(proj_act, K)
            ax_his(0)
            for n, col in enumerate(FIRST):
                task(0, -1, "", col, counts=[K + n, n, n, 0])
                if col != VCOL:
                    rope_hi(0, -1, "", col, counts=[K + n, n, n, 0])
            run_steps(act, step)

        for u in range(z.UF):
            weights_hi(0, u)
        ffn(0)
        if attn:
            attention()
        if ffn2:
            for u in range(z.UF):
                if u == 0:
                    act.wait_ge(xadd_done, B * UB)
                weights_hi(1, u)
            ffn(B)

    @block.vector
    def _(dve):
        def link(ins):
            ins.then_inc(stat_step, 1)
            chain["n"] += 1
            dve.wait_ge(stat_step, chain["n"] + chain["loop"])

        def norm(n, b):
            for t in range(T):
                norm_stats(b, t)
            rsqrt_start()
            for _ in range(3):
                rsqrt_step()
            for t in range(T):
                ins = nc.vector.tensor_scalar(work[:, t * D:(t + 1) * D], xb(b, t), mv[:, 0, t:t + 1], rs[:, 1, t:t + 1],
                                              ALU.subtract, ALU.mult)
            ins.then_inc(xn_done, 1)

        def xb(b, t):
            return x[:, b, t] if type(b) is int else x[:, bass.ds(b, 1), t].rearrange("p a d -> p (a d)")

        def x_lo(n):
            for k in range(K):
                dve.wait_ge(xh_done, K * n + k + 1)
                nc.vector.tensor_tensor(xl[:, k], xf[:, k], xh[:, k].bitcast(F32), ALU.subtract).then_inc(xl_done, 1)

        def bc(a):
            return a.rearrange("p (t o) -> p t o", o=1).broadcast_to([P, T, E])

        rev = revidx[:].rearrange("p (o e) -> p o e", o=1).broadcast_to([P, T, E])

        def route_shift(n):
            dve.wait_ge(logit_done, n + 1)
            L = ps[:, LOG, 0:T * E].rearrange("p (t e) -> p t e", t=T)
            link(nc.vector.tensor_reduce(lm[:, 0], L, AX_X, ALU.max))
            nc.vector.tensor_tensor(lg[:, 0], L, bc(lm[:, 0]), ALU.subtract).then_inc(lshift_done, 1)

        def pick(e, m, eq, oh):
            link(nc.vector.tensor_reduce(m, e, AX_X, ALU.max))
            link(nc.vector.tensor_tensor(eq, e, bc(m), ALU.is_ge))
            link(nc.vector.tensor_tensor(eq, eq, rev, ALU.mult))
            link(nc.vector.tensor_reduce(lm[:, 2], eq, AX_X, ALU.max))
            link(nc.vector.tensor_tensor(oh, eq, bc(lm[:, 2]), ALU.is_ge))

        def route_first(n):
            dve.wait_ge(lexp_done, n + 1)
            pick(lg[:, 1], lm[:, 0], lg[:, 2], lg[:, 3])
            link(nc.vector.scalar_tensor_tensor(lg[:, 0], lg[:, 3], -4.0, lg[:, 1], ALU.mult, ALU.add))

        def route_second(n):
            pick(lg[:, 0], lm[:, 1], lg[:, 2], lg[:, 4])

        def route_parts(n):
            link(nc.vector.tensor_tensor(lg[:, 3], lg[:, 3], lg[:, 4], ALU.add))
            link(nc.vector.tensor_tensor(lg[:, 3], lg[:, 3], lg[:, 1], ALU.mult))
            link(nc.vector.tensor_tensor(lm[:, 3], lm[:, 0], lm[:, 1], ALU.add))
            link(nc.vector.reciprocal(lm[:, 3], lm[:, 3]))
            link(nc.vector.tensor_tensor(lg[:, 0], lg[:, 3], bc(lm[:, 3]), ALU.mult))
            link(nc.vector.tensor_copy(comb[:, :, 0:E], lg[:, 0]))
            link(nc.vector.tensor_tensor(lg[:, 2], lg[:, 0], comb[:, :, 0:E], ALU.subtract))
            link(nc.vector.tensor_copy(comb[:, :, E:2 * E], lg[:, 2]))
            link(nc.vector.tensor_tensor(lg[:, 4], lg[:, 2], comb[:, :, E:2 * E], ALU.subtract))
            nc.vector.tensor_copy(comb[:, :, 2 * E:3 * E], lg[:, 4]).then_inc(comb_done, 1)

        def norm_stats(b, t):
            nc.vector.bn_stats(stats[:, t], xb(b, t)).then_inc(stat_step, 1)
            chain["n"] += 1

        def rsqrt_start():
            dve.wait_ge(stat_step, chain["n"] + chain["loop"])
            v, y, b2 = rs[:, 0], rs[:, 1], rs[:, 3]
            mean_e, m2_e, mean_o, m2_o = (stats[:, :, i] for i in (1, 2, 4, 5))
            nc.vector.tensor_tensor(mv[:, 1], mean_e, mean_o, ALU.add).then_inc(stat_step, 1)
            nc.vector.tensor_tensor(mv[:, 2], mean_e, mean_o, ALU.subtract).then_inc(stat_step, 1)
            nc.vector.tensor_tensor(mv[:, 3], m2_e, m2_o, ALU.add).then_inc(stat_step, 1)
            chain["n"] += 3
            dve.wait_ge(stat_step, chain["n"] + chain["loop"])
            nc.vector.tensor_scalar(mv[:, 0], mv[:, 1], 0.5, None, ALU.mult).then_inc(stat_step, 1)
            nc.vector.scalar_tensor_tensor(mv[:, 4], mv[:, 2], 0.25, mv[:, 2], ALU.mult, ALU.mult).then_inc(stat_step, 1)
            chain["n"] += 2
            dve.wait_ge(stat_step, chain["n"] + chain["loop"])
            link(nc.vector.scalar_tensor_tensor(v, mv[:, 3], 1.0 / D, mv[:, 4], ALU.mult, ALU.add))
            link(nc.vector.tensor_scalar(v, v, EPS, None, ALU.add))
            link(nc.vector.tensor_scalar(b2.bitcast(I32), v.bitcast(I32), 1, None, ALU.logical_shift_right))
            link(nc.vector.tensor_scalar(y.bitcast(I32), b2.bitcast(I32), -1.0, float(0x5F3759DF), ALU.mult, ALU.add))

        def rsqrt_step():
            v, y, a, b2 = rs[:, 0], rs[:, 1], rs[:, 2], rs[:, 3]
            link(nc.vector.tensor_tensor(a, y, y, ALU.mult))
            link(nc.vector.scalar_tensor_tensor(b2, a, -0.5, v, ALU.mult, ALU.mult))
            link(nc.vector.scalar_tensor_tensor(y, b2, 1.5, y, ALU.add, ALU.mult))

        def normalise(b):
            for t in range(T):
                ins = nc.vector.tensor_scalar(work[:, t * D:(t + 1) * D], xb(b, t), mv[:, 0, t:t + 1], rs[:, 1, t:t + 1],
                                              ALU.subtract, ALU.mult)
            ins.then_inc(axn_done, 1)

        def ax_los(b):
            for kk in range(K):
                dve.wait_ge(ax_hi, K * b + kk + 1)
                nc.vector.tensor_tensor(xl[:, kk], xf[:, kk], xh[:, kk].bitcast(F32), ALU.subtract).then_inc(ax_lo, 1)

        def task(b, k, place, col, counts=None):
            if col < 0:
                return
            c = counts or [JB[i] * b + v for i, v in enumerate(task_count(k, place, col))]
            g = k // T + 1
            if col == VCOL:
                dve.wait_ge(proj_act, c[0] + 1)
                nc.vector.tensor_tensor(v_at(g, 1), ps[:, JBANK], v_at(g, 0).bitcast(F32), ALU.subtract).then_inc(proj_dve, 1)
                return
            dve.wait_ge(proj_done, c[0] + 1)
            dve.wait_ge(q_lo, c[2])
            nc.vector.scalar_tensor_tensor(ropeA[:], ps[:, JBANK], 1.0 if col == KCOL else SCALE, cos[:],
                                           ALU.mult, ALU.mult).then_inc(proj_dve, 1)

        def maximum(b, k, h):
            i = k % T
            m = b * UB * G + k * G + h
            dve.wait_ge(s_done, m + 1)
            if not (type(b) is int and b == 0 and k < 2):
                dve.wait_ge(exp_done, m - 2 * G + 1)
            nc.vector.tensor_reduce(nmax[:, k % 2, h:h + 1], ps[:, bank_of((k * G + h) % (UB * G)), 0:(i + 1) * P],
                                    AX_X, ALU.max, negate=True).then_inc(nmax_done, 1)

        def pt_los(b, k, j):
            n = b * PB + tiles_before(k) + j
            dve.wait_ge(pt_hi, n + 1)
            nc.vector.tensor_tensor(pT_at(tiles_before(k) + j, 1), ps[:, TBANK + (tiles_before(k) + j) % 2],
                                    pT_at(tiles_before(k) + j, 0).bitcast(F32), ALU.subtract).then_inc(pt_lo, 1)

        def divide(b, k):
            i = k % T
            dve.wait_ge(exp_done, b * UB * G + (k + 1) * G)
            nc.vector.reciprocal(rinv[:, k % 2], ssum[:, k % 2]).then_inc(recip_done, 1)
            dve.wait_ge(recip_done, b * UB + k + 1)
            for h in range(G):
                p = prob[k % 2][:, h, 0:(i + 1) * P]
                ins = nc.vector.tensor_scalar(p, p, rinv[:, k % 2, h:h + 1], None, ALU.mult)
            ins.then_inc(norm_done, 1)

        def a_los(b, k):
            dve.wait_ge(a_hi, b * UB + k + 1)
            nc.vector.tensor_tensor(a_at(k, 1), ps[:, OBANK], a_at(k, 0).bitcast(F32), ALU.subtract).then_inc(a_lo, 1)

        def x_add(b, k):
            dve.wait_ge(wo_done, b * UB + k + 1)
            if not (type(b) is int and b == 0 and k == 0):
                dve.wait_ge(xadd_done, b * UB + k)
            xs = xb(b + k // UB, k % T)
            nc.vector.tensor_tensor(xs, xs, ps[:, WBANK, 0:D], ALU.add).then_inc(xadd_done, 1)

        def step(b, k, scores, values, tasks):
            i, ip = k % T, (k - 1) % T
            jobs = tasks_at(k, tasks)
            if k % UB == LAST_GROUP and tasks is True:
                dve.wait_ge(proj_done, JN * (b + k // UB) + task_count(LAST_GROUP - 1, "end", VCOL)[0] + 1)
                ax_los(b + 1)
            for h in range(G):
                if scores:
                    maximum(b, k, h)
                if h == 0 and k >= 2:
                    x_add(b, k - 2)
                if h >= 1 and values and h - 1 <= ip:
                    pt_los(b, k - 1, h - 1)
                if h == 1:
                    for place, col in jobs:
                        if place == "mid":
                            task(b, k, place, col)
            if values and ip >= G - 1:
                pt_los(b, k - 1, G - 1)
            if scores:
                divide(b, k)
            if values:
                a_los(b, k - 1)
            for place, col in jobs:
                if place == "end":
                    task(b, k, place, col)
            if tasks is True and LN_AT - 6 <= k < LN_AT:
                n = k - (LN_AT - 6)
                if n < T:
                    norm_stats(b + 1, n)
                elif n == T:
                    rsqrt_start()
                    rsqrt_step()
                else:
                    rsqrt_step()
                    rsqrt_step()
                    dve.wait_ge(proj_done, JN * b + K)
                    normalise(b + 1)

        def attention():
            dve.wait_ge(down_done, B * NC)
            dve.wait_ge(lo_done, B * NC)
            dve.wait_ge(tab_in, 32)
            dve.wait_ge(x_done, B)
            for t in range(T):
                norm_stats(0, t)
            rsqrt_start()
            for _ in range(3):
                rsqrt_step()
            normalise(0)
            ax_los(0)
            for n, col in enumerate(FIRST):
                task(0, -1, "", col, counts=[K + n, n, n, 0])
            chain["loop"] = 0
            for k in range(PEEL):
                step(0, k, True, k > 0, True)
            per, PER2 = chain["n"], T + 9 + 9
            with dve.Fori(0, B - 1) as b:
                chain["loop"] = b * PER2
                for k in range(PEEL, UB + PEEL):
                    step(b, k, True, True, True)
            assert chain["n"] - per == PER2
            chain["n"] += (B - 2) * PER2
            chain["loop"] = 0
            for k in range(PEEL, UB):
                step(B - 1, k, True, True, "own")
            step(B - 1, UB, False, True, False)
            step(B - 1, UB + 1, False, False, False)

        def h(n, c):
            cc = n * NC + c
            s = stage[:, 2 + c % 2]
            dve.wait_ge(silu_done, cc + 1)
            dve.wait_ge(up_done, cc + 1)
            nc.vector.tensor_tensor(s, s, ps[:, UP], ALU.mult).then_inc(su_done, 1)
            dve.wait_ge(su_done, cc + 1)
            dve.wait_ge(cb_done, cc + 1)
            nc.vector.tensor_tensor(s, s, ps[:, CB], ALU.mult).then_inc(h_done, 1)

        def first(n, b):
            norm(n, b)
            x_lo(n)
            route_shift(n)
            route_first(n)
            route_second(n)
            route_parts(n)

        def batch(n, b, last):
            for c in range(1, NC + 1):
                if c < NC or not last:
                    if c == NC:
                        dve.wait_ge(up_done, (n + 1) * NC)
                        x_lo(n + 1)
                    h(n, c) if c < NC else h(n + 1, 0)
                if not last:
                    if c == 2:
                        norm(n + 1, b + 1)
                    if c == 6:
                        route_shift(n + 1)
                    if c == 7:
                        route_first(n + 1)
                    if c == 8:
                        route_second(n + 1)
                    if c == 9:
                        dve.wait_ge(combT_ps, n + 1)
                        route_parts(n + 1)
            dve.wait_ge(ffn_back, n + 1)
            xs = x[:, b].rearrange("p t d -> p (t d)") if type(b) is int else \
                x[:, bass.ds(b, 1)].rearrange("p a t d -> p (a t d)")
            nc.vector.tensor_tensor(xs, xs, ps[:, MISC:MISC + 2].rearrange("p a c -> p (a c)"), ALU.add).then_inc(x_done, 1)

        def ffn(n0):
            first(n0, 0)
            h(n0, 0)
            per = chain["n"]
            with dve.Fori(0, B - 1) as b:
                chain["loop"] = b * PER
                batch(b + n0, b, False)
            assert chain["n"] - per == PER, chain["n"] - per
            chain["n"] += (B - 2) * PER
            chain["loop"] = 0
            batch(n0 + B - 1, B - 1, True)

        PER = T + 9 + 9 + 1 + 6 + 5 + 9

        nc.vector.memset(comb[:], 0.0).then_inc(comb_zero, 1)
        dve.wait_ge(comb_zero, 1)
        dve.wait_ge(x_in, 16 * B)
        dve.wait_ge(const_in, 96)
        def weights_lo(turn):
            for u in range(0, z.UF, 2):
                dve.wait_ge(w_hi, turn * z.UF + u + 1)
                nc.vector.tensor_tensor(ffn_w(turn, u, 1), stage[:, u % 4], ffn_w(turn, u, 0).bitcast(F32), ALU.subtract)\
                  .then_inc(w_lo_d, 1)

        weights_lo(0)
        ffn(0)
        if attn:
            attention()
        if ffn2:
            dve.wait_ge(xadd_done, B * UB)
            dve.wait_ge(refill, 16)
            nc.vector.memset(comb[:], 0.0).then_inc(comb_zero, 1)
            dve.wait_ge(comb_zero, 2)
            weights_lo(1)
            ffn(B)

    @block.gpsimd
    def _(pool):
        def h_lo(n, c):
            cc = n * NC + c
            pool.wait_ge(hi_done, cc + 1)
            if not (type(n) is int and cc < 2):
                pool.wait_ge(down_done, n * NC + (c - 1 if c != 1 else 1))
            nc.gpsimd.tensor_tensor(hl[:, c % 2], stage[:, 2 + c % 2], hh[:, c % 2].bitcast(F32), ALU.subtract).then_inc(lo_done, 1)

        def batch(turn, n, last):
            for c in range(1, NC + (0 if last else 1)):
                h_lo(n, c) if c < NC else h_lo(n + 1, 0)
                if turn == 0 and attn and c % 2 and c // 2 < AU:
                    attn_w_lo(n, c // 2)

        def attn_w_lo(b, j):
            pool.wait_ge(aw_hi, b * AU + j + 1)
            at = (b * AU + j) * 2
            hi, lo = (wA[:, at + q] if type(b) is int else wA[:, bass.ds(at + q, 1)].rearrange("p a c -> p (a c)") for q in (0, 1))
            nc.gpsimd.tensor_tensor(lo, stage[:, j % 2], hi.bitcast(F32), ALU.subtract).then_inc(aw_lo, 1)

        def ffn(n0):
            h_lo(n0, 0)
            with pool.Fori(n0, n0 + B - 1) as n:
                batch(n0 // B, n, False)
            batch(n0 // B, n0 + B - 1, True)

        def weights_lo(turn):
            for u in range(1, z.UF, 2):
                pool.wait_ge(w_hi, turn * z.UF + u + 1)
                nc.gpsimd.tensor_tensor(ffn_w(turn, u, 1), stage[:, u % 4], ffn_w(turn, u, 0).bitcast(F32), ALU.subtract)\
                  .then_inc(w_lo_p, 1)

        def rope(b, k, place, col, counts=None):
            if col < 0 or col == VCOL:
                return
            c = counts or [JB[i] * b + v for i, v in enumerate(task_count(k, place, col))]
            g = k // T + 1
            pool.wait_ge(proj_act, c[0] + 1)
            nc.gpsimd.tensor_tensor(ropeB[:], ropeB[:], sin[:], ALU.mult).then_inc(rope_mul, 1)
            pool.wait_ge(rope_mul, c[2] + 1)
            pool.wait_ge(proj_dve, c[1] + 1)
            nc.gpsimd.tensor_tensor(ropeA[:], ropeA[:], ropeB[:], ALU.add).then_inc(rope_sum, 1)
            pool.wait_ge(q_hi, c[2] + 1)
            hi, lo = (k_at(g, q) if col == KCOL else q_at(g, col, q) for q in (0, 1))
            nc.gpsimd.tensor_tensor(lo, ropeA[:], hi.bitcast(F32), ALU.subtract).then_inc(q_lo, 1)

        def step(b, k, scores, values, tasks):
            for place, col in tasks_at(k, tasks):
                rope(b, k, place, col)

        weights_lo(0)
        ffn(0)
        if attn:
            pool.wait_ge(tab_in, 32)
            for n, col in enumerate(FIRST):
                rope(0, -1, "", col, counts=[K + n, n, n, 0])
            run_steps(pool, step)
        if ffn2:
            weights_lo(1)
            ffn(B)

    @block.tensor
    def _(pe):
        def mm(out, lhsT, rhs, start, stop, **kw):
            return nc.tensor.matmul(out, lhsT, rhs, start=start, stop=stop, **kw)

        def transposes(n):
            pe.wait_ge(xn_done, n + 1)
            for k in range(K):
                for t in range(T):
                    ins = nc.tensor.transpose(ps[:, MISC + k, t * P:(t + 1) * P],
                                              work[:, t * D + k * P:t * D + (k + 1) * P], ident[:])
            ins.then_inc(xnT_done, 1)

        def route(n):
            pe.wait_ge(xf_done, n + 1)
            for t in range(T):
                for k in range(K):
                    ins = mm(ps[:, LOG, t * E:(t + 1) * E], xf[:, k, t * P:(t + 1) * P], router[:, k], k == 0, k == K - 1)
            ins.then_inc(logit_done, 1)

        def comb_transposes(n):
            pe.wait_ge(comb_done, n + 1)
            for t in range(T):
                ins = nc.tensor.transpose(ps[:, LOG].bitcast(BF16)[:, t * P:(t + 1) * P], comb[:, t], identb[:])
            ins.then_inc(combT_ps, 1)

        def gate_up(wt, n, c):
            cc = n * NC + c
            for which, bank, free, done in ((0, GATE, silu_done, gate_done), (1, UP, su_done, up_done)):
                if not (type(n) is int and cc == 0):
                    pe.wait_ge(free, cc)
                if c == 0:
                    pe.wait_ge(xh_done, K * n + K)
                o = ps[:, bank]
                for k in range(K):
                    mm(o, gu_w(wt, c, which, k, 0), xh[:, k], k == 0, False)
                    mm(o, gu_w(wt, c, which, k, 1), xh[:, k], False, False)
                if c == 0:
                    pe.wait_ge(xl_done, K * n + K)
                for k in range(K):
                    ins = mm(o, gu_w(wt, c, which, k, 0), xl[:, k], False, k == K - 1)
                ins.then_inc(done, 1)
            if not (type(n) is int and cc == 0):
                pe.wait_ge(h_done, cc)
            if c == 0:
                pe.wait_ge(combT_done, n + 1)
            mm(ps[:, CB], expand[:, c * P:(c + 1) * P], combT[:], True, True).then_inc(cb_done, 1)

        def down(wt, base, n, c):
            cc = n * NC + c
            pe.wait_ge(lo_done, cc + 1)
            for k in range(K):
                o = ps[:, DOWN + k]
                mm(o, down_w(wt, base, c, k, 0), hh[:, c % 2], c == 0, False)
                mm(o, down_w(wt, base, c, k, 1), hh[:, c % 2], False, False)
                ins = mm(o, down_w(wt, base, c, k, 0), hl[:, c % 2], False, c == NC - 1)
            ins.then_inc(down_done, 1)

        def batch(wt, wd, base, n, last):
            for c in range(1, NC + 1):
                if c < NC:
                    gate_up(wt, n, c)
                elif not last:
                    comb_transposes(n + 1)
                    gate_up(wt, n + 1, 0)
                down(wd, base, n, c - 1)
                if not last:
                    if c == 3:
                        transposes(n + 1)
                    if c == 5:
                        pe.wait_ge(combT_done, n + 1)
                        route(n + 1)
            pe.wait_ge(ffn_evac, n + 1)
            for t in range(T):
                for k in range(K):
                    at = (t % 2) * D + k * P
                    ins = nc.tensor.transpose(ps[:, MISC + t // 2, at:at + P], work[:, k * S + t * P:k * S + (t + 1) * P], ident[:])
            ins.then_inc(ffn_back, 1)

        def ffn(wt, wd, base, n0):
            transposes(n0)
            route(n0)
            comb_transposes(n0)
            gate_up(wt, n0, 0)
            with pe.Fori(n0, n0 + B - 1) as n:
                batch(wt, wd, base, n, False)
            batch(wt, wd, base, n0 + B - 1, True)

        def bank_free(c):
            pe.wait_ge(proj_act, c[0])
            pe.wait_ge(proj_dve, c[1])

        def ax_transposes(b, kk, c):
            pe.wait_ge(axn_done, b + 1)
            bank_free(c)
            for t in range(T):
                ins = nc.tensor.transpose(ps[:, JBANK, t * P:(t + 1) * P], work[:, t * D + kk * P:t * D + (kk + 1) * P], ident[:])
            ins.then_inc(proj_done, 1)

        def task(b, k, place, col, counts=None):
            c = counts or [JB[i] * b + v for i, v in enumerate(task_count(k, place, col))]
            if col < 0:
                return ax_transposes(b + 1, -1 - col, c)
            bank_free(c)
            g = (k // T + 1) % KV
            bx = b + (k // T + 1) // KV
            pe.wait_ge(ax_lo, K * bx + K)
            if col == VCOL:
                for t in range(T):
                    o, tok = ps[:, JBANK, t * P:(t + 1) * P], slice(t * P, (t + 1) * P)
                    for kk in range(K):
                        mm(o, xh[:, kk, tok], qkv_w(g, col, kk, 0), kk == 0, False)
                        mm(o, xh[:, kk, tok], qkv_w(g, col, kk, 1), False, False)
                        ins = mm(o, xl[:, kk, tok], qkv_w(g, col, kk, 0), False, kk == K - 1)
            else:
                o = ps[:, JBANK]
                for kk in range(K):
                    mm(o, qkv_w(g, col, kk, 0), xh[:, kk], kk == 0, False)
                    mm(o, qkv_w(g, col, kk, 1), xh[:, kk], False, False)
                    ins = mm(o, qkv_w(g, col, kk, 0), xl[:, kk], False, kk == K - 1)
            ins.then_inc(proj_done, 1)

        def scores_of(b, k, h):
            g, i = divmod(k, T)
            m = k * G + h
            if not (type(b) is int and b == 0 and m < 3):
                pe.wait_ge(exp_done, b * UB * G + m - bank_before(m) + 1)
            if h == 0 and i == 0:
                pe.wait_ge(q_lo, (G + 1) * (KV * b + g) + 1)
            if i == 0:
                pe.wait_ge(q_lo, (G + 1) * (KV * b + g) + 2 + h)
            o = ps[:, bank_of(m % (UB * G)), 0:(i + 1) * P]
            rows = slice(i * P, (i + 1) * P)
            mm(o, q_at(g, h, 0)[:, rows], k_at(g, 0)[:, 0:(i + 1) * P], True, False)
            mm(o, q_at(g, h, 0)[:, rows], k_at(g, 1)[:, 0:(i + 1) * P], False, False)
            mm(o, q_at(g, h, 1)[:, rows], k_at(g, 0)[:, 0:(i + 1) * P], False, False)
            mm(o[:, rows], identb[:], causal[:], False, True).then_inc(s_done, 1)

        def prob_transposes(b, k, j):
            tb = tiles_before(k) + j
            pe.wait_ge(norm_done, b * UB + k + 1)
            if not (type(b) is int and b == 0 and tb < 2):
                pe.wait_ge(pt_lo, b * PB + tb - 1)
            for h in range(G):
                ins = nc.tensor.transpose(ps[:, TBANK + tb % 2, h * P:(h + 1) * P], prob[k % 2][:, h, j * P:(j + 1) * P], ident[:])
            ins.then_inc(pt_done, 1)

        def values_of(b, k, j):
            g, i = divmod(k, T)
            tb = tiles_before(k) + j
            pe.wait_ge(pt_lo, b * PB + tb + 1)
            if j == 0:
                if not (type(b) is int and b == 0 and k == 0):
                    pe.wait_ge(a_lo, b * UB + k)
                if i == 0:
                    pe.wait_ge(proj_dve, (G + 2) * (KV * b + g) + G + 2)
            keys = slice(j * P, (j + 1) * P)
            o = ps[:, OBANK]
            mm(o, v_at(g, 0)[:, keys], pT_at(tb, 0), j == 0, False)
            mm(o, v_at(g, 1)[:, keys], pT_at(tb, 0), False, False)
            mm(o, v_at(g, 0)[:, keys], pT_at(tb, 1), False, j == i).then_inc(pv_done, 1)

        def project(b, k):
            g = (k // T) % KV
            pe.wait_ge(a_lo, b * UB + k + 1)
            if not (type(b) is int and b == 0 and k == 0):
                pe.wait_ge(xadd_done, b * UB + k)
            o = ps[:, WBANK, 0:D]
            for h in range(G):
                rows = slice(h * P, (h + 1) * P)
                mm(o, a_at(k, 0)[:, rows], wo_w(g, h, 0), h == 0, False)
                mm(o, a_at(k, 0)[:, rows], wo_w(g, h, 1), False, False)
                ins = mm(o, a_at(k, 1)[:, rows], wo_w(g, h, 0), False, h == G - 1)
            ins.then_inc(wo_done, 1)

        def step(b, k, scores, values, tasks):
            ip = (k - 1) % T
            jobs = tasks_at(k, tasks)
            if k >= 2:
                project(b, k - 2)
            for h in range(G):
                if scores:
                    scores_of(b, k, h)
                if h >= 1 and values and h - 1 <= ip:
                    prob_transposes(b, k - 1, h - 1)
                if h >= 2 and values and h - 2 <= ip:
                    values_of(b, k - 1, h - 2)
                if h == 1:
                    for place, col in jobs:
                        if place == "mid":
                            task(b, k, place, col)
            if values:
                if ip >= G - 1:
                    prob_transposes(b, k - 1, G - 1)
                for j in (G - 2, G - 1):
                    if j <= ip:
                        values_of(b, k - 1, j)
            for place, col in jobs:
                if place == "end":
                    task(b, k, place, col)

        def attention():
            pe.wait_ge(x_done, B)
            pe.wait_ge(aw_lo, z.UA)
            for kk in range(K):
                ax_transposes(0, kk, [kk, 0])
            for n, col in enumerate(FIRST):
                task(0, -1, "", col, counts=[K + n, n, n, 0])
            run_steps(pe, step)

        pe.wait_ge(const_in, 96)
        pe.wait_ge(w_lo_d, z.UF // 2)
        pe.wait_ge(w_lo_p, z.UF // 2)
        ffn(wF, wF, z.UG, 0)
        if attn:
            attention()
        if ffn2:
            pe.wait_ge(w_lo_d, z.UF // 2 * 2)
            pe.wait_ge(w_lo_p, z.UF // 2 * 2)
            ffn(wA, wF, z.UG, B)


def layouts(L0_attn_x, L0_attn_Wqkv, L0_attn_Wo, L0_ffn_router_w, L0_ffn_gate_w, L0_ffn_up_w, L0_ffn_down_w):
    f = np.float32
    x, wqkv, wo, rw, gw, uw, dw = (np.asarray(a) for a in (
        L0_attn_x, L0_attn_Wqkv, L0_attn_Wo, L0_ffn_router_w, L0_ffn_gate_w, L0_ffn_up_w, L0_ffn_down_w))
    z = Sizes(x.shape, wqkv.shape, wo.shape, rw.shape, gw.shape)
    B, S, D, T, K, H, KV, G = z.B, z.S, z.D, z.T, z.K, z.H, z.KV, z.G
    gu = [w.transpose(1, 0, 2).reshape(K, P, z.NC, P).transpose(2, 1, 0, 3) for w in (gw, uw)]
    gu = np.concatenate(gu, axis=2).reshape(z.UG, P, 512)
    dn = dw.reshape(z.UD, 2, P, D).transpose(0, 2, 1, 3).reshape(z.UD, P, 512)
    w = wqkv.reshape(K, P, H + 2 * KV, P)
    heads = [j for g in range(KV) for j in [*range(G * g, G * g + G), H + g, H + KV + g]]
    qkv = w[:, :, heads].reshape(K, P, z.UQ, 2, P).transpose(2, 1, 3, 0, 4).reshape(z.UQ, P, 512)
    won = wo.reshape(z.UO, 2, P, D).transpose(0, 2, 1, 3).reshape(z.UO, P, 512)
    half = P // 2
    freqs = (f(1.0) / f(10000.0) ** (np.arange(0, P, 2, dtype=f) / f(P))).astype(f)
    ang = np.arange(S, dtype=f)[None, :] * freqs[:, None]
    expand = np.zeros((P, z.EF), f)
    for r in range(3 * z.E):
        e = r % z.E
        expand[r, e * z.F:(e + 1) * z.F] = 1
    return z, {
        "x": np.ascontiguousarray(x.reshape(B, T, P, D).transpose(0, 2, 1, 3)),
        "wffn": np.ascontiguousarray(np.concatenate([gu, dn])),
        "wattn": np.ascontiguousarray(np.concatenate([qkv, won])),
        "router": np.ascontiguousarray(rw.reshape(K, P, z.E).transpose(1, 0, 2)),
        "revidx": np.tile(np.arange(z.E, 0, -1, dtype=f), (P, 1)),
        "ident": np.eye(P, dtype=f),
        "identb": np.eye(P, dtype=f).astype(np.dtype("bfloat16")),
        "expand": expand.astype(np.dtype("bfloat16")),
        "causal": np.triu(np.full((P, P), -2.3819763e38, f), k=1).astype(np.dtype("bfloat16")),
        "cos": np.concatenate([np.cos(ang), np.cos(ang)]).astype(f),
        "sin": np.concatenate([-np.sin(ang), np.sin(ang)]).astype(f),
    }


def kernel(**inputs):
    import concourse.bacc as bacc
    from concourse.bass_utils import run_bass_kernel_spmd

    z, arrays = layouts(**inputs)
    arrays = {f"in_{name}": a for name, a in arrays.items()}
    nc = bacc.Bacc("TRN2", target_bir_lowering=False, num_devices=1)
    dram = {name[3:]: nc.dram_tensor(name, a.shape, mybir.dt.from_np(a.dtype), kind="ExternalInput").ap()
            for name, a in arrays.items()}
    dram["out"] = nc.dram_tensor("out_y", (z.B, P, z.T, z.D), F32, kind="ExternalOutput").ap()
    build(nc, dram, z)
    y = run_bass_kernel_spmd(nc, [arrays], core_ids=[0]).results[0]["out_y"]
    return y.transpose(0, 2, 1, 3).reshape(z.B, z.S, z.D)
```

```python
from contextlib import ExitStack

import concourse.bass as bass
import numpy as np
from concourse import mybir

F32 = mybir.dt.float32
F32R = mybir.dt.float32r
BF16 = mybir.dt.bfloat16
I32 = mybir.dt.int32
ALU = mybir.AluOpType
ACT = mybir.ActivationFunctionType
AX_X = mybir.AxisListType.X

P = 128
EPS = 1e-5


class Sizes:

    def __init__(self, x, wqkv, wo, router, gate):
        self.B, self.S, self.D = x
        self.E, _, self.F = gate
        self.EF = self.E * self.F
        self.NC = self.EF // P
        self.T = self.S // P
        self.K = self.D // P
        self.H = wo[0] // P
        self.KV = (wqkv[1] // P - self.H) // 2
        self.G = self.H // self.KV
        self.UG = self.NC
        self.UD = self.NC // 2
        self.QE = 4
        self.FC = P // self.QE
        self.CQ = self.F // self.FC
        self.NQ = self.E // self.QE
        self.UF = self.UG + self.UD
        self.UQ = self.KV * 3
        self.UO = self.H // 2
        self.UA = self.UQ + self.UO


def build(nc, A, z):
    with ExitStack() as ctx:
        program(nc, A, z, ctx)


def program(nc, A, z, ctx):
    B, S, D, E, T, K, NC, G, KV = z.B, z.S, z.D, z.E, z.T, z.K, z.NC, z.G, z.KV

    def sb(name, shape, dt, at=ctx):
        return at.enter_context(nc.sbuf_tensor("sb_" + name, shape, dt))

    def sem(name):
        return ctx.enter_context(nc.semaphore(name))

    wF = sb("wF", [P, 2 * z.UF, 512], F32R)
    wA = sb("wA", [P, 2 * z.UA, 512], F32R)
    x = sb("x", [P, B, T, D], F32)
    xf = sb("xf", [P, K, S], F32)
    xh = sb("xh", [P, K, S], F32R)
    xl = sb("xl", [P, K, S], F32R)
    work = sb("work", [P, T * D], F32)
    ident = sb("ident", [P, P], F32)
    identb = sb("identb", [P, P], BF16)
    causal = sb("causal", [P, P], BF16)
    router = sb("router", [P, K, E], F32)
    revidx = sb("revidx", [P, E], F32)
    stats = sb("stats", [P, T, 6], F32)
    mv = sb("mv", [P, 5, T], F32)
    rs = sb("rs", [P, 4, T], F32)

    with ExitStack() as own:
        stage = sb("stage", [P, 4, 512], F32, own)
        hh = sb("hh", [P, 2, 512], F32R, own)
        hl = sb("hl", [P, 2, 512], F32R, own)
        expand = sb("expand", [P, z.NQ * P], BF16, own)
        sb("gap", [P, 2 * P], F32, own)
        combT = sb("combT", [P, S], BF16, own)
        comb = sb("comb", [P, T, P], BF16, own)
        lg = sb("lg", [P, 5, T, E], F32, own)
        lm = sb("lm", [P, 4, T], F32, own)
    own = ctx.enter_context(ExitStack())
    cos = sb("cos", [P, S], F32, own)
    sin = sb("sin", [P, S], F32, own)
    prob1 = sb("prob1", [P, G, S], F32, own)
    prob0 = sb("prob0", [P, G, S - P], F32, own)
    prob = [prob0, prob1]
    ropeB = sb("ropeB", [P, 2, S], F32, own)
    nmax = sb("nmax", [P, 2, G], F32, own)
    ssum = sb("ssum", [P, 2, G], F32, own)
    rinv = sb("rinv", [P, 4, G], F32, own)

    ps = ctx.enter_context(nc.psum_tensor("ps", [P, 8, 512], F32))
    GATE, UP, CB, DOWN, MISC, LOG = 0, 1, 2, 3, 5, 7

    raw_in = [sem(f"raw_in{i}") for i in range(4)]
    x_in = [sem(f"x_in{b}") for b in range(B)]
    w_hi = sem("w_hi")
    w_lo = sem("w_lo")
    ident_in = sem("ident_in")
    router_in = sem("router_in")
    const_in = sem("const_in")
    tab_in = sem("tab_in")
    refill = sem("refill")
    out_done = sem("out_done")
    gate_done = sem("gate_done")
    up_done = sem("up_done")
    cb_done = sem("cb_done")
    down_done = sem("down_done")
    silu_done = sem("silu_done")
    sc_done = sem("sc_done")
    h_done = sem("h_done")
    hi_done = sem("hi_done")
    lo_done = sem("lo_done")
    stat_step = sem("stat_step")
    xn_done = sem("xn_done")
    xnT_done = sem("xnT_done")
    xf_done = sem("xf_done")
    xh_done = sem("xh_done")
    xl_done = sem("xl_done")
    logit_done = sem("logit_done")
    lshift_done = sem("lshift_done")
    lexp_done = sem("lexp_done")
    comb_done = sem("comb_done")
    combT_ps = sem("combT_ps")
    combT_done = sem("combT_done")
    ffn_evac = sem("ffn_evac")
    ffn_back = sem("ffn_back")
    x_done = sem("x_done")
    comb_zero = sem("comb_zero")
    bxT_done = sem("bxT_done")
    bxf_done = sem("bxf_done")
    bx_hi = sem("bx_hi")
    bx_lo = sem("bx_lo")
    ax_hi = sem("ax_hi")
    ax_lo = sem("ax_lo")
    axn_done = sem("axn_done")
    proj_done = sem("proj_done")
    proj_act = sem("proj_act")
    proj_dve = sem("proj_dve")
    rope_mul = sem("rope_mul")
    rope_sum = sem("rope_sum")
    q_hi = sem("q_hi")
    q_lo = sem("q_lo")
    s_done = sem("s_done")
    nmax_done = sem("nmax_done")
    exp_done = sem("exp_done")
    recip_done = sem("recip_done")
    pt_done = sem("pt_done")
    pt_hi = sem("pt_hi")
    pt_lo = sem("pt_lo")
    pv_done = sem("pv_done")
    a_hi = sem("a_hi")
    a_lo = sem("a_lo")
    wo_done = sem("wo_done")
    xadd_done = sem("xadd_done")

    UB = KV * T
    PB = KV * T * (T + 1) // 2
    SBANK, TBANK, OBANK, WBANK, JBANK = 0, 3, 5, 6, 7

    def tiles_before(k):
        g, i = divmod(k, T)
        return g * T * (T + 1) // 2 + i * (i + 1) // 2

    def bank_of(m):
        return SBANK + (1 if m == UB * G - 1 else m % 3)

    def bank_before(m):
        M = UB * G
        return next(d for d in range(1, 9) if bank_of((m - d) % M) == bank_of(m % M))

    KCOL, VCOL, VALUES = G, G + 1, G + 2
    LAST_GROUP = UB - T
    LN_GROUP = KV - 2

    ORDER = {
        "pe": """
        S,0,0 S,0,1 T,-1,0 V,-2,2 W,-3,1 T,-1,1 J,0,4 S,0,2 V,-1,0 T,-1,2 S,0,3 V,-1,1 W,-2,0 T,-1,3 S,1,0 S,1,1
        V,-1,2 J,0,0 W,-2,1 V,-1,3 T,0,0 S,1,2 S,1,3 S,2,0 J,0,1 W,-1,0 V,0,0 T,1,0 S,2,1 S,2,2 W,-1,1 J,0,2
        T,1,1 S,2,3 V,1,0 W,0,0 S,3,0 J,0,3 W,0,1 T,2,0 V,1,1 S,3,1 J,0,5 T,2,1 S,3,2 V,2,0 J,0,6 S,3,3 T,2,2
        W,1,0 V,2,1""",
        "act": """
        pt_hi,-1,0 exp,0,0 exp,0,1 a_hi,-2,0 pt_hi,-1,1 Ja,0,4 pt_hi,-1,2 exp,0,2 exp,0,3 pt_hi,-1,3 exp,1,0
        rope_hi,0,4 exp,1,1 Ja,0,0 a_hi,-1,0 pt_hi,0,0 exp,1,2 exp,1,3 rope_hi,0,0 exp,2,0 Ja,0,1 pt_hi,1,0
        exp,2,1 a_hi,0,0 exp,2,2 pt_hi,1,1 rope_hi,0,1 Ja,0,2 exp,2,3 exp,3,0 Ja,0,3 rope_hi,0,2 pt_hi,2,0
        a_hi,1,0 exp,3,1 Ja,0,5 pt_hi,2,1 exp,3,2 Ja,0,6 rope_hi,0,3 pt_hi,2,2 exp,3,3""",
        "dve": """
        pt_lo,-2,2 x_add2,-3,0 max,0,0 recip,-1,0 max,0,1 pt_lo,-1,0 x_add,-3,1 a_lo,-2,0 x_add2,-3,1 pt_lo,-1,1
        Jd,0,4 max,0,2 max,0,3 pt_lo,-1,2 x_add,-2,0 max,1,0 x_add2,-2,0 pt_lo,-1,3 recip,0,0 max,1,1 Jd,0,0
        x_add,-2,1 x_add2,-2,1 max,1,2 a_lo,-1,0 pt_lo,0,0 max,1,3 max,2,0 Jd,0,1 x_add,-1,0 recip,1,0
        x_add2,-1,0 max,2,1 max,2,2 pt_lo,1,0 x_add,-1,1 a_lo,0,0 x_add2,-1,1 Jd,0,2 max,2,3 pt_lo,1,1 x_add,0,0
        x_add2,0,0 max,3,0 recip,2,0 Jd,0,3 x_add,0,1 x_add2,0,1 max,3,1 pt_lo,2,0 a_lo,1,0 max,3,2 pt_lo,2,1
        max,3,3 Jd,0,6 x_add,1,0""",
        "pool": """
        PM,0,4 PL,0,4 PM,0,0 PL,0,0 PM,0,1 PL,0,1 PM,0,2 PL,0,2 PM,0,3 PL,0,3""",
    }

    ORDER_LAST = {
        "pe": """
        S,0,0 S,0,1 T,-1,0 V,-2,2 W,-3,1 T,-1,1 S,0,2 T,-1,2 S,0,3 S,1,0 V,-1,0 W,-2,0 V,-1,1 T,-1,3 V,-1,2
        W,-2,1 S,1,1 T,0,0 V,-1,3 S,1,2 S,1,3 S,2,0 W,-1,0 V,0,0 T,1,0 S,2,1 W,-1,1 S,2,2 T,1,1 V,1,0 S,2,3
        W,0,0 S,3,0 V,1,1 S,3,1 T,2,0 W,0,1 T,2,1 S,3,2 S,3,3 V,2,0 T,2,2 W,1,0 V,2,1 W,1,1 T,3,0 V,2,2 T,3,1
        T,3,2 V,3,0 V,3,1 W,2,0 T,3,3 V,3,2 W,2,1 V,3,3 W,3,0 W,3,1""",
        "act": """
        pt_hi,-1,0 exp,0,0 exp,0,1 a_hi,-2,0 pt_hi,-1,1 pt_hi,-1,2 exp,0,2 exp,0,3 pt_hi,-1,3 exp,1,0 pt_hi,0,0
        exp,1,1 a_hi,-1,0 exp,1,2 exp,1,3 exp,2,0 a_hi,0,0 pt_hi,1,0 pt_hi,1,1 exp,2,1 exp,2,2 exp,2,3 a_hi,1,0
        exp,3,0 pt_hi,2,0 exp,3,1 pt_hi,2,1 exp,3,2 pt_hi,2,2 exp,3,3 pt_hi,3,0 a_hi,2,0 pt_hi,3,1 pt_hi,3,2
        pt_hi,3,3 a_hi,3,0""",
        "dve": """
        pt_lo,-2,2 x_add2,-3,0 max,0,0 recip,-1,0 max,0,1 pt_lo,-1,0 x_add,-3,1 a_lo,-2,0 x_add2,-3,1 pt_lo,-1,1
        max,0,2 pt_lo,-1,2 max,0,3 x_add,-2,0 max,1,0 x_add2,-2,0 recip,0,0 pt_lo,-1,3 x_add,-2,1 max,1,1
        x_add2,-2,1 pt_lo,0,0 max,1,2 a_lo,-1,0 max,1,3 max,2,0 x_add,-1,0 recip,1,0 x_add2,-1,0 a_lo,0,0
        pt_lo,1,0 x_add,-1,1 max,2,1 x_add2,-1,1 max,2,2 pt_lo,1,1 max,2,3 x_add,0,0 max,3,0 x_add2,0,0
        recip,2,0 max,3,1 a_lo,1,0 x_add,0,1 pt_lo,2,0 x_add2,0,1 pt_lo,2,1 max,3,2 max,3,3 x_add,1,0 x_add2,1,0
        pt_lo,2,2 recip,3,0 x_add,1,1 x_add2,1,1 pt_lo,3,0 a_lo,2,0 pt_lo,3,1 pt_lo,3,2 x_add,2,0 x_add2,2,0
        pt_lo,3,3 x_add,2,1 x_add2,2,1 a_lo,3,0 x_add,3,0 x_add2,3,0 x_add,3,1 x_add2,3,1""",
        "pool": "",
    }

    def group_order(engine, g, table=None):
        out, due = [], carried.get((engine, g - 1), [])
        for item in (table or ORDER)[engine].split():
            what, unit, n = item.split(",")
            k, n = int(unit) + g * T, int(n)
            out.append((what, k, n))
            due = [(wait - 1, w) for wait, w in due]
            if what == "recip" and 0 <= k - LN_FROM < LN_STEPS:
                out.append(("ln", k, k - LN_FROM))
            if g == LN_GROUP and what in ("J", "Ja", "Jd") and n == VALUES:
                due = [(after, (what, k, -1 - kk)) for kk, after in enumerate(AX_AFTER[what])]
                due += {"J": [], "Ja": [(due[-1][0], ("ax_hi", k, 0))], "Jd": [(due[-1][0], ("ax_lo", k, 0))]}[what]
            out += [w for wait, w in due if wait == 0]
            due = [(wait, w) for wait, w in due if wait > 0]
        carried[engine, g] = due
        return out

    TASKS_FROM = NC - 3
    AX_AFTER = {"J": (2, 4), "Ja": (1, 3), "Jd": (1, 3)}
    LN_STEPS = 8
    LN_FROM = LAST_GROUP - 1 - LN_STEPS
    carried = {}

    order = [(k, n) for g in range(KV) for w, k, n in group_order("pe", g) if w == "J"]
    JN = len(order)
    JB = JN, (G + 1) * KV, JN - KV
    FIRST = [KCOL, *range(G), VCOL, VALUES]

    def task_count(k, col):
        more, k = divmod(k, UB)
        n = order.index((k, col))
        ropes = sum(0 <= c < VCOL for _, c in order[:n])
        dv = sum(c != VCOL for _, c in order[:n])
        return G + 3 + more * JB[0] + n, G + 1 + more * JB[1] + ropes, G + 2 + more * JB[2] + dv

    def first_counts(r):
        return [r, min(r, G + 1), min(r, G + 1)]

    def values_use(g):
        if g == 0:
            return G + 2
        n = next(n for n, (k, c) in enumerate(order) if c == VALUES and k // T == g - 1)
        return G + 2 + sum(c != VCOL for _, c in order[:n + 1])

    def bank_of_task(k, c):
        return JBANK if k >= 0 or c[0] % 2 == 0 else CB if c[0] == G + 1 else MISC + 1

    def rope_slot(col):
        return FIRST.index(col) % 2

    def slot_left(col):
        return 0 if col == KCOL else 1

    PT_SLOT, A_SLOT = 2 * (G + 2), 2 * (G + 2) + 8

    def set_base(g):
        return 0 if g % 2 == 0 else 2 * z.UG

    def q_at(g, h, part):
        return wF[:, set_base(g) + 2 * h + part]

    def k_at(g, part):
        return wF[:, set_base(g) + 2 * G + part]

    def v_at(g, part):
        return wF[:, set_base(g) + 2 * G + 2 + part]

    def pT_at(n, part):
        return wF[:, PT_SLOT + 2 * (n % 4) + part]

    def a_at(k, part):
        return wF[:, A_SLOT + 2 * (k % 2) + part]

    def bx_at(kk, part):
        return wF[:, PT_SLOT + K * part + kk]

    def qkv_w(g, col, k, part):
        at = (col % 2) * D + k * P
        return wA[:, 2 * (3 * g + col // 2) + part, at:at + P]

    def wo_w(g, h, part):
        hq = G * g + h
        at = (hq % 2) * D
        return wA[:, 2 * (z.UQ + hq // 2) + part, at:at + D]

    SCALE = float(P) ** -0.5
    HP = P // 2

    BY_USE = [u for q in range(z.UD) for u in (2 * q, 2 * q + 1, z.UG + q)]
    AU = -(-z.UA // (B - 1))

    def stage_slot(p):
        return p if p < 4 else p % 2

    def attn_units(b):
        return min(AU, z.UA - AU * (b - 1))

    LANDED = [sum(stage_slot(p) == i for p in range(z.UF)) for i in (0, 1)]
    LANDED_A = [len(range(i, AU, 2)) for i in (0, 1)]
    LANDED_ALL = [LANDED[i] + sum(len(range(i, attn_units(b), 2)) for b in range(1, B)) for i in (0, 1)]

    def head_of(engine):
        return [(w, k, n) for w, k, n in group_order(engine, 0) if k >= 0]

    def turn_of(engine):
        return [i for g in range(1, KV + 1) for i in group_order(engine, g) if i[0] not in ("ax_hi", "ax_lo")]

    EXTRA = {
        "pe": {("V", UB - T - 1, T - 2): "route", ("T", UB - 1, 1): "comb_T", ("V", UB - 1, T - 2): "gates",
               ("V", UB - 1, T - 1): "combine"},
        "act": {("exp", UB - 3, 1): "logit_exp", ("pt_hi", UB - 1, 1): "combT", ("pt_hi", UB - 1, T - 1): "silu",
                ("a_hi", UB - 1, 0): "h_hi"},
        "dve": {("max", UB - 3, 1): "shift", ("max", UB - 2, 0): "first", ("pt_lo", UB - 3, 1): "second",
                ("recip", UB - 2, 0): "parts", ("max", UB - 1, 1): "parts2", ("a_lo", UB - 1, 0): "h"},
        "pool": {},
    }

    RELOAD = {1: [(6, 0, 8)], 2: [(3, 0, 2)], 3: [(3, 1, 3), (6, 3, 7)]}

    def tail_of(engine):
        out, u = [], 0
        for g in range(1, KV):
            items = [i for i in group_order(engine, g, ORDER_LAST if g == KV - 1 else None) if not (i[0] == "Jd" and i[2] < 0)]
            if engine in ("act", "pool"):
                at = [len(items) * (start * more + (end - start) * j) // (8 * more)
                      for more, start, end in RELOAD[g] for j in range(more)]
                for j, a in enumerate(at):
                    items.insert(a + j, ("reload", 0, u))
                    u += 1
            for i in items:
                out.append(i)
                if i in EXTRA[engine]:
                    out.append((EXTRA[engine][i], 0, 0))
        assert engine in ("pe", "dve") or u == z.UF
        assert sum(i[0] in EXTRA[engine].values() for i in out) == len(EXTRA[engine])
        return out

    def attn_w(b, j, part):
        at = (b * AU + j - AU) * 2 + part
        return wA[:, at] if type(b) is int else wA[:, bass.ds(at, 1)].rearrange("p a c -> p (a c)")

    def ffn_w(turn, u, part):
        if turn == 0:
            return wF[:, 2 * u + part]
        return wA[:, 2 * u + part] if u < z.UG else wF[:, 2 * (u - z.UG) + part]

    EARLY = z.UG * 3 // 4
    SPLIT_AT = {2: (7, 8), 3: (9,), 4: (10, 11), 5: (12,), 6: (13, 14), 7: (15,), 8: (16,), 9: (17,)}
    SPLIT = z.UF + z.UA

    def reload_slot(u):
        return work[:, (u % 2) * 512:(u % 2) * 512 + 512] if u < EARLY else stage[:, u % 2]

    def projected(g):
        return G + 3 + JN * (B - 1) + sum(n >= 0 and k < g * T for k, n in order)

    AX_AT = [next(i for i, (k, n) in enumerate(order) if n == -1 - kk) for kk in range(K)]
    assert AX_AT[-1] <= JN - (G + 4)

    def gu_w(wt, c, which, k, part):
        at = (2 * which + k) * P
        return wt[:, 2 * c + part, at:at + P]

    def down_w(wt, base, c, k, part):
        at = (c % 2) * D + k * P
        return wt[:, 2 * (base + c // 2) + part, at:at + P]

    chain = {"n": 0, "loop": 0}

    block = ctx.enter_context(nc.Block())

    @block.sync
    def _(sp):
        sp.dma_start(x[:, 0], A["x"][0]).then_inc(x_in[0], 16)
        sp.dma_start(ident[:], A["ident"]).then_inc(ident_in, 16)
        sp.dma_start(router[:], A["router"]).then_inc(router_in, 16)
        sp.dma_start(stage[:, 0], A["wffn"][BY_USE[0]]).then_inc(raw_in[0], 16)
        sp.dma_start(revidx[:], A["revidx"]).then_inc(const_in, 16)
        sp.dma_start(identb[:], A["identb"]).then_inc(const_in, 16)
        sp.dma_start(expand[:], A["expand"]).then_inc(const_in, 16)
        for p in range(1, z.UF):
            if p >= 4:
                sp.wait_ge(w_lo, p - 1 if p > 5 else p - 3)
            sp.dma_start(stage[:, stage_slot(p)], A["wffn"][BY_USE[p]]).then_inc(raw_in[stage_slot(p)], 16)
            if p == 3:
                sp.dma_start(x[:, 1], A["x"][1]).then_inc(x_in[1], 16)
                sp.dma_start(causal[:], A["causal"]).then_inc(const_in, 16)
        for b in range(2, B):
            sp.dma_start(x[:, b], A["x"][b]).then_inc(x_in[b], 16)
        for b in range(1, B):
            for j in range(attn_units(b)):
                i = AU * (b - 1) + j
                sp.wait_ge(w_lo, z.UF + i - (j > 0))
                sp.dma_start(stage[:, j % 2], A["wattn"][i]).then_inc(raw_in[j % 2], 16)
        sp.wait_ge(w_lo, z.UF + z.UA)
        sp.dma_start(cos[:], A["cos"]).then_inc(tab_in, 16)
        sp.dma_start(sin[:], A["sin"]).then_inc(tab_in, 16)
        for u in range(z.UF):
            if u == 0:
                sp.wait_ge(proj_done, G + 3 + JN * (B - 2) + AX_AT[-1] + 1)
            elif u == EARLY:
                sp.wait_ge(q_lo, (G + 1) * KV * B)
            if u % EARLY >= 2:
                sp.wait_ge(w_lo, SPLIT + u - 1)
            sp.dma_start(reload_slot(u), A["wffn"][u]).then_inc(raw_in[u % 2], 16)
        sp.wait_ge(pt_done, (B - 1) * PB + tiles_before(UB - 1))
        sp.dma_start(expand[:], A["expand"]).then_inc(refill, 16)
        for b in range(B):
            sp.wait_ge(x_done, B + b + 1)
            sp.dma_start(A["out"][b], x[:, b]).then_inc(out_done, 16)
        sp.wait_ge(out_done, 16 * B)

    @block.scalar
    def _(act):
        def weights_hi(p):
            i = stage_slot(p)
            act.wait_ge(raw_in[i], 16 * sum(stage_slot(q) == i for q in range(p + 1)))
            nc.scalar.activation(ffn_w(0, BY_USE[p], 0), stage[:, i], ACT.Copy).then_inc(w_hi, 1)

        def reload_hi(u):
            act.wait_ge(raw_in[u % 2], 16 * (LANDED_ALL[u % 2] + u // 2 + 1))
            if u < z.UG:
                act.wait_ge(proj_done, projected(u // 3))
            else:
                act.wait_ge(pv_done, (B - 1) * PB + tiles_before(LAST_GROUP))
            nc.scalar.activation(ffn_w(1, u, 0), reload_slot(u), ACT.Copy).then_inc(w_hi, 1)

        def attn_w_hi(b, j):
            act.wait_ge(raw_in[j % 2], 16 * (LANDED_A[j % 2] * b + LANDED[j % 2] - LANDED_A[j % 2] + j // 2 + 1))
            nc.scalar.activation(attn_w(b, j, 0), stage[:, j % 2], ACT.Copy).then_inc(w_hi, 1)

        def xf_copy(n):
            act.wait_ge(xnT_done, n + 1)
            if not (type(n) is int and n % B == 0):
                act.wait_ge(logit_done, n)
                act.wait_ge(xl_done, K * n)
            nc.scalar.activation(xf[:], ps[:, MISC:MISC + 2], ACT.Copy).then_inc(xf_done, 1)

        def x_hi(n):
            for k in range(K):
                nc.scalar.activation(xh[:, k], xf[:, k], ACT.Copy).then_inc(xh_done, 1)

        def logit_exp(n):
            act.wait_ge(lshift_done, n + 1)
            nc.scalar.activation(lg[:, 1], lg[:, 0], ACT.Exp).then_inc(lexp_done, 1)

        def combT_copy(n):
            act.wait_ge(combT_ps, n + 1)
            nc.scalar.activation(combT[:], ps[:, LOG].bitcast(BF16)[:, 0:S], ACT.Copy).then_inc(combT_done, 1)

        def silu(n, c):
            cc = n * NC + c
            act.wait_ge(gate_done, cc + 1)
            if not (type(n) is int and cc < 2):
                act.wait_ge(lo_done, cc - 1)
            nc.scalar.activation(stage[:, 2 + c % 2], ps[:, GATE], ACT.Silu).then_inc(silu_done, 1)

        def h_hi(n, c):
            cc = n * NC + c
            act.wait_ge(h_done, cc + 1)
            if not (type(n) is int and cc < 2):
                act.wait_ge(down_done, cc - 1)
            nc.scalar.activation(hh[:, c % 2], stage[:, 2 + c % 2], ACT.Copy).then_inc(hi_done, 1)

        def first(n):
            xf_copy(n)
            act.wait_ge(xf_done, n + 1)
            x_hi(n)
            logit_exp(n)

        def evacuate(n):
            act.wait_ge(down_done, (n + 1) * NC)
            nc.scalar.activation(work[:], ps[:, DOWN:DOWN + 2], ACT.Copy, scale=0.5).then_inc(ffn_evac, 1)

        def batch(turn, n, last, start=False):
            for c in range(2, NC):
                silu(n, c)
                if c == NC - 1 and not last:
                    act.wait_ge(up_done, (n + 1) * NC)
                    act.wait_ge(xf_done, n + 2)
                    x_hi(n + 1)
                if turn == 0 and not start and c - 2 < (attn_units(n) if last else AU):
                    attn_w_hi(n, c - 2)
                if c == 6 and not last:
                    xf_copy(n + 1)
                if c == 8 and not last:
                    logit_exp(n + 1)
                if turn == 0 and last:
                    bridge(c)
                h_hi(n, c)
                if start:
                    for p in SPLIT_AT.get(c, []):
                        weights_hi(p)
                if turn == 0 and last and c >= TASKS_FROM:
                    task(0, -1, FIRST[c - TASKS_FROM], counts=first_counts(c - TASKS_FROM))
            if last and turn == 0:
                bridge_end(n)
                return
            if last:
                evacuate(n)
                return
            act.wait_ge(cb_done, (n + 1) * z.NQ)
            combT_copy(n + 1)
            silu(n + 1, 0)
            h_hi(n + 1, 0)
            evacuate(n)
            silu(n + 1, 1)
            h_hi(n + 1, 1)

        def bridge(c):
            if c == 6:
                act.wait_ge(bxT_done, 1)
                act.wait_ge(logit_done, B)
                act.wait_ge(xl_done, K * B)
                nc.scalar.activation(xf[:], ps[:, MISC:MISC + 2], ACT.Copy).then_inc(bxf_done, 1)
            if c == 8:
                act.wait_ge(bxf_done, 1)
                act.wait_ge(up_done, (B - 1) * NC + c)
                for kk in range(K):
                    nc.scalar.activation(bx_at(kk, 0), xf[:, kk], ACT.Copy).then_inc(bx_hi, 1)
            if c > TASKS_FROM:
                r = c - TASKS_FROM - 1
                rope_hi(0, -1, FIRST[r], counts=first_counts(r))

        def bridge_end(n):
            act.wait_ge(up_done, (n + 1) * NC)
            for kk in range(K):
                nc.scalar.activation(xh[:, kk], bx_at(kk, 0).bitcast(F32), ACT.Copy).then_inc(ax_hi, 1)
            for r in range(NC - TASKS_FROM, G + 1):
                task(0, -1, FIRST[r], counts=first_counts(r))
                rope_hi(0, -1, FIRST[r - 1], counts=first_counts(r - 1))
                if r == G - 1:
                    evacuate(n)
            task(0, -1, VCOL, counts=first_counts(G + 1))
            task(0, -1, VALUES, counts=first_counts(G + 2))
            rope_hi(0, -1, FIRST[G], counts=first_counts(G))

        def ffn(n0):
            if n0 == 0:
                first(n0)
                act.wait_ge(w_lo, 3)
                silu(n0, 0)
                weights_hi(4)
                combT_copy(n0)
                h_hi(n0, 0)
                act.wait_ge(w_lo, 4)
            silu(n0, 1)
            if n0 == 0:
                weights_hi(5)
            h_hi(n0, 1)
            if n0 == 0:
                weights_hi(6)
                batch(0, 0, False, start=True)
            with act.Fori(n0 or 1, n0 + B - 1) as n:
                batch(n0 // B, n, False)
            batch(n0 // B, n0 + B - 1, True)

        def ax_part(b, kk, n):
            act.wait_ge(proj_done, n + 1)
            nc.scalar.activation(xh[:, kk], ps[:, JBANK], ACT.Copy).then_inc(proj_act, 1)

        def ax_copy(kk, n):
            if kk == 0:
                act.wait_ge(q_lo, (G + 1) * KV * B)
                act.wait_ge(proj_done, n + 1)
            else:
                act.wait_ge(xnT_done, B + 1)
            nc.scalar.activation(xf[:, kk], ps[:, JBANK], ACT.Copy).then_inc(xf_done if kk else proj_act, 1)

        def task(b, k, col, counts=None):
            c = counts or [JB[i] * b + v for i, v in enumerate(task_count(k, col))]
            bank = bank_of_task(k, c)
            if col < 0:
                return ax_copy(-1 - col, c[0]) if type(b) is int and b == B - 1 else ax_part(b, -1 - col, c[0])
            g = k // T + 1
            act.wait_ge(proj_done, c[0] + 1)
            if col == VCOL:
                act.wait_ge(rope_sum, c[1] - slot_left(col))
                nc.scalar.activation(ropeB[:, rope_slot(col)], ps[:, bank], ACT.Copy).then_inc(proj_act, 1)
                return
            if col == VALUES:
                if k >= 0:
                    act.wait_ge(pv_done, b * PB + max(tiles_before(g * T - T), 1))
                nc.scalar.activation(v_at(g, 0), ps[:, bank], ACT.Copy).then_inc(proj_act, 1)
                return
            r = c[1]
            if type(r) is int and r == 0:
                act.wait_ge(cb_done, B * z.NQ)
            if not (type(r) is int and r < 2):
                act.wait_ge(rope_sum, r - slot_left(col))
            act.wait_ge(proj_dve, c[2] + 1)
            scale = 1.0 if col == KCOL else SCALE
            slot = rope_slot(col)
            nc.scalar.activation(ropeB[0:HP, slot], ps[HP:P, bank], ACT.Copy, scale=scale)
            nc.scalar.activation(ropeB[HP:P, slot], ps[0:HP, bank], ACT.Copy, scale=scale).then_inc(proj_act, 1)

        def rope_hi(b, k, col, counts=None):
            c = counts or [JB[i] * b + v for i, v in enumerate(task_count(k, col))]
            g = k // T + 1
            act.wait_ge(rope_sum, c[1] + 1)
            if k >= 0:
                act.wait_ge(s_done, b * UB * G + max((g - 1) * T * G, 1))
            dst = k_at(g, 0) if col == KCOL else q_at(g, col, 0)
            nc.scalar.activation(dst, xf[:, rope_slot(col)], ACT.Copy).then_inc(q_hi, 1)

        def exp(b, k, h):
            i = k % T
            m = b * UB * G + k * G + h
            act.wait_ge(nmax_done, m + 1)
            if not (type(b) is int and b == 0 and k < 2):
                act.wait_ge(pt_done, b * PB + tiles_before(k - 1))
            nc.scalar.activation(prob[k % 2][:, h, 0:(i + 1) * P], ps[:, bank_of((k * G + h) % (UB * G)), 0:(i + 1) * P],
                                 ACT.Exp, bias=nmax[:, k % 2, h:h + 1], accum_out=ssum[:, k % 2, h:h + 1]).then_inc(exp_done, 1)

        def pt_his(b, k, j):
            n = b * PB + tiles_before(k) + j
            act.wait_ge(pt_done, n + 1)
            if not (type(b) is int and b == 0 and tiles_before(k) + j < 4):
                act.wait_ge(pv_done, b * PB + max(tiles_before(k) + j - 3, 1))
            nc.scalar.activation(pT_at(tiles_before(k) + j, 0), ps[:, TBANK + (tiles_before(k) + j) % 2], ACT.Copy)\
              .then_inc(pt_hi, 1)

        def a_his(b, k):
            act.wait_ge(pv_done, b * PB + tiles_before(k + 1))
            if not (type(b) is int and b == 0 and k < 2):
                act.wait_ge(wo_done, (G // 2) * (b * UB + k - 1))
            nc.scalar.activation(a_at(k, 0), ps[:, OBANK], ACT.Copy).then_inc(a_hi, 1)

        def do(b, items):
            for what, k, n in items:
                if what == "exp":
                    exp(b, k, n)
                elif what == "pt_hi":
                    pt_his(b, k, n)
                elif what == "a_hi":
                    a_his(b, k)
                elif what == "Ja":
                    task(b, k, n)
                elif what == "rope_hi":
                    rope_hi(b, k, n)
                elif what == "ax_hi":
                    act.wait_ge(xf_done, B + 1)
                    x_hi(B)
                elif what == "reload":
                    reload_hi(n)
                elif what == "logit_exp":
                    logit_exp(B)
                elif what == "combT":
                    act.wait_ge(q_lo, (G + 1) * KV * B)
                    combT_copy(B)
                elif what == "silu":
                    silu(B, 0)
                elif what == "h_hi":
                    h_hi(B, 0)

        for p in range(4):
            weights_hi(p)
        ffn(0)
        do(0, head_of("act"))
        with act.Fori(0, B - 1) as b:
            do(b, turn_of("act"))
        do(B - 1, tail_of("act"))
        ffn(B)

    @block.vector
    def _(dve):
        def link(ins):
            ins.then_inc(stat_step, 1)
            chain["n"] += 1
            dve.wait_ge(stat_step, chain["n"] + chain["loop"])

        def norm(n, b):
            for t in range(T):
                norm_stats(b, t)
            mean_start()
            rsqrt_start()
            for _ in range(3):
                rsqrt_step()
            normalise(b, 0, xn_done)
            normalise(b, 2, xn_done)

        def normalise(b, t0, done):
            for t in (t0, t0 + 1):
                ins = nc.vector.tensor_scalar(work[:, t * D:(t + 1) * D], xb(b, t), mv[:, 0, t:t + 1], rs[:, 1, t:t + 1],
                                              ALU.subtract, ALU.mult)
            ins.then_inc(done, 1)

        def xb(b, t):
            b = b % B if type(b) is int else b
            return x[:, b, t] if type(b) is int else x[:, bass.ds(b, 1), t].rearrange("p a d -> p (a d)")

        def x_lo(n):
            for k in range(K):
                dve.wait_ge(xh_done, K * n + k + 1)
                nc.vector.tensor_tensor(xl[:, k], xf[:, k], xh[:, k].bitcast(F32), ALU.subtract).then_inc(xl_done, 1)

        def bc(a):
            return a.rearrange("p (t o) -> p t o", o=1).broadcast_to([P, T, E])

        rev = revidx[:].rearrange("p (o e) -> p o e", o=1).broadcast_to([P, T, E])

        def route_shift(n):
            dve.wait_ge(logit_done, n + 1)
            L = ps[:, LOG, 0:T * E].rearrange("p (t e) -> p t e", t=T)
            link(nc.vector.tensor_reduce(lm[:, 0], L, AX_X, ALU.max))
            nc.vector.tensor_tensor(lg[:, 0], L, bc(lm[:, 0]), ALU.subtract).then_inc(lshift_done, 1)

        def pick(e, m, eq, oh):
            link(nc.vector.tensor_reduce(m, e, AX_X, ALU.max))
            link(nc.vector.tensor_tensor(eq, e, bc(m), ALU.is_ge))
            link(nc.vector.tensor_tensor(eq, eq, rev, ALU.mult))
            link(nc.vector.tensor_reduce(lm[:, 2], eq, AX_X, ALU.max))
            link(nc.vector.tensor_tensor(oh, eq, bc(lm[:, 2]), ALU.is_ge))

        def route_first(n):
            dve.wait_ge(lexp_done, n + 1)
            pick(lg[:, 1], lm[:, 0], lg[:, 2], lg[:, 3])
            link(nc.vector.scalar_tensor_tensor(lg[:, 0], lg[:, 3], -4.0, lg[:, 1], ALU.mult, ALU.add))

        def route_second(n):
            pick(lg[:, 0], lm[:, 1], lg[:, 2], lg[:, 4])

        def route_weights():
            link(nc.vector.tensor_tensor(lg[:, 3], lg[:, 3], lg[:, 4], ALU.add))
            link(nc.vector.tensor_tensor(lg[:, 3], lg[:, 3], lg[:, 1], ALU.mult))
            link(nc.vector.tensor_tensor(lm[:, 3], lm[:, 0], lm[:, 1], ALU.add))
            link(nc.vector.reciprocal(lm[:, 3], lm[:, 3]))
            link(nc.vector.tensor_tensor(lg[:, 0], lg[:, 3], bc(lm[:, 3]), ALU.mult))

        def route_parts():
            link(nc.vector.tensor_copy(comb[:, :, 0:E], lg[:, 0]))
            link(nc.vector.tensor_tensor(lg[:, 2], lg[:, 0], comb[:, :, 0:E], ALU.subtract))
            link(nc.vector.tensor_copy(comb[:, :, E:2 * E], lg[:, 2]))
            link(nc.vector.tensor_tensor(lg[:, 4], lg[:, 2], comb[:, :, E:2 * E], ALU.subtract))
            nc.vector.tensor_copy(comb[:, :, 2 * E:3 * E], lg[:, 4]).then_inc(comb_done, 1)

        def norm_stats(b, t):
            nc.vector.bn_stats(stats[:, t], xb(b, t)).then_inc(stat_step, 1)
            chain["n"] += 1

        def mean_start():
            dve.wait_ge(stat_step, chain["n"] + chain["loop"])
            mean_e, m2_e, mean_o, m2_o = (stats[:, :, i] for i in (1, 2, 4, 5))
            nc.vector.tensor_tensor(mv[:, 1], mean_e, mean_o, ALU.add).then_inc(stat_step, 1)
            nc.vector.tensor_tensor(mv[:, 2], mean_e, mean_o, ALU.subtract).then_inc(stat_step, 1)
            nc.vector.tensor_tensor(mv[:, 3], m2_e, m2_o, ALU.add).then_inc(stat_step, 1)
            chain["n"] += 3
            dve.wait_ge(stat_step, chain["n"] + chain["loop"])
            nc.vector.tensor_scalar(mv[:, 0], mv[:, 1], 0.5, None, ALU.mult).then_inc(stat_step, 1)
            nc.vector.scalar_tensor_tensor(mv[:, 4], mv[:, 2], 0.25, mv[:, 2], ALU.mult, ALU.mult).then_inc(stat_step, 1)
            chain["n"] += 2

        def rsqrt_start():
            v, y, b2 = rs[:, 0], rs[:, 1], rs[:, 3]
            dve.wait_ge(stat_step, chain["n"] + chain["loop"])
            link(nc.vector.scalar_tensor_tensor(v, mv[:, 3], 1.0 / D, mv[:, 4], ALU.mult, ALU.add))
            link(nc.vector.tensor_scalar(v, v, EPS, None, ALU.add))
            link(nc.vector.tensor_scalar(b2.bitcast(I32), v.bitcast(I32), 1, None, ALU.logical_shift_right))
            link(nc.vector.tensor_scalar(y.bitcast(I32), b2.bitcast(I32), -1.0, float(0x5F3759DF), ALU.mult, ALU.add))

        def rsqrt_step():
            v, y, a, b2 = rs[:, 0], rs[:, 1], rs[:, 2], rs[:, 3]
            link(nc.vector.tensor_tensor(a, y, y, ALU.mult))
            link(nc.vector.scalar_tensor_tensor(b2, a, -0.5, v, ALU.mult, ALU.mult))
            link(nc.vector.scalar_tensor_tensor(y, b2, 1.5, y, ALU.add, ALU.mult))

        def task(b, k, col, counts=None):
            c = counts or [JB[i] * b + v for i, v in enumerate(task_count(k, col))]
            g = k // T + 1
            bank = bank_of_task(k, c)
            if col < 0:
                dve.wait_ge(proj_act, c[0] + 1)
                nc.vector.tensor_tensor(xl[:, -1 - col], ps[:, bank], xh[:, -1 - col].bitcast(F32), ALU.subtract)\
                  .then_inc(proj_dve, 1)
                return
            if col == VALUES:
                dve.wait_ge(proj_act, c[0] + 1)
                nc.vector.tensor_tensor(v_at(g, 1), ps[:, bank], v_at(g, 0).bitcast(F32), ALU.subtract).then_inc(proj_dve, 1)
                return
            dve.wait_ge(proj_done, c[0] + 1)
            r = c[1]
            if not (type(r) is int and r < 2):
                dve.wait_ge(q_lo, r - slot_left(col))
            nc.vector.scalar_tensor_tensor(xf[:, rope_slot(col)], ps[:, bank], 1.0 if col == KCOL else SCALE, cos[:],
                                           ALU.mult, ALU.mult).then_inc(proj_dve, 1)

        def maximum(b, k, h):
            i = k % T
            m = b * UB * G + k * G + h
            dve.wait_ge(s_done, m + 1)
            if not (type(b) is int and b == 0 and k < 2):
                dve.wait_ge(exp_done, m - 2 * G + 1)
            nc.vector.tensor_reduce(nmax[:, k % 2, h:h + 1], ps[:, bank_of((k * G + h) % (UB * G)), 0:(i + 1) * P],
                                    AX_X, ALU.max, negate=True).then_inc(nmax_done, 1)

        def pt_los(b, k, j):
            n = b * PB + tiles_before(k) + j
            dve.wait_ge(pt_hi, n + 1)
            nc.vector.tensor_tensor(pT_at(tiles_before(k) + j, 1), ps[:, TBANK + (tiles_before(k) + j) % 2],
                                    pT_at(tiles_before(k) + j, 0).bitcast(F32), ALU.subtract).then_inc(pt_lo, 1)

        def reciprocal_sum(b, k):
            dve.wait_ge(exp_done, b * UB * G + (k + 1) * G)
            if not (type(b) is int and b == 0 and k < 4):
                dve.wait_ge(xadd_done, G * UB * b + G * (k - 3))
            nc.vector.reciprocal(rinv[:, k % 4], ssum[:, k % 2]).then_inc(recip_done, 1)

        def a_los(b, k):
            dve.wait_ge(a_hi, b * UB + k + 1)
            nc.vector.tensor_tensor(a_at(k, 1), ps[:, OBANK], a_at(k, 0).bitcast(F32), ALU.subtract).then_inc(a_lo, 1)

        def x_add(b, k, h):
            dve.wait_ge(wo_done, (G // 2) * (b * UB + k) + h // 2 + 1)
            dve.wait_ge(recip_done, b * UB + k + 1)
            if not (type(b) is int and b == 0 and k == 0 and h == 0):
                dve.wait_ge(xadd_done, G * (b * UB + k) + h)
            xs = xb(b + k // UB, k % T)
            at = (h % 2) * D
            nc.vector.scalar_tensor_tensor(xs, ps[:, WBANK, at:at + D], rinv[:, k % 4, h:h + 1], xs,
                                           ALU.mult, ALU.add).then_inc(xadd_done, 1)

        def do(b, items):
            for what, k, n in items:
                if what == "max":
                    maximum(b, k, n)
                elif what == "recip":
                    reciprocal_sum(b, k)
                elif what == "pt_lo":
                    pt_los(b, k, n)
                elif what == "a_lo":
                    a_los(b, k)
                elif what in ("x_add", "x_add2"):
                    x_add(b, k, 2 * n + (what == "x_add2"))
                elif what == "Jd":
                    task(b, k, n)
                elif what == "ax_lo":
                    x_lo(B)
                elif what == "ln":
                    last = type(b) is int and b == B - 1
                    if n < 2:
                        norm_stats(b + 1, 2 * n)
                        norm_stats(b + 1, 2 * n + 1)
                    elif n == 2:
                        mean_start()
                    elif n == 3:
                        rsqrt_start()
                    elif n < 6:
                        for _ in range(n - 3):
                            rsqrt_step()
                    else:
                        if n == 6 and last:
                            dve.wait_ge(w_lo, SPLIT + EARLY)
                        elif n == 6:
                            dve.wait_ge(proj_done, JN * b + 1)
                        normalise(b + 1, 2 * n - 12, xn_done if last else axn_done)
                elif what == "shift":
                    dve.wait_ge(q_lo, (G + 1) * KV * B)
                    link(nc.vector.memset(comb[:], 0.0))
                    route_shift(B)
                elif what == "first":
                    route_first(B)
                elif what == "second":
                    route_second(B)
                elif what == "parts":
                    route_weights()
                elif what == "parts2":
                    route_parts()
                elif what == "h":
                    h(B, 0)

        def attention():
            chain["loop"] = 0
            do(0, head_of("dve"))
            per, PER2 = chain["n"], T + 9 + 9
            with dve.Fori(0, B - 1) as b:
                chain["loop"] = b * PER2
                do(b, turn_of("dve"))
            assert chain["n"] - per == PER2
            chain["n"] += (B - 2) * PER2
            chain["loop"] = 0
            do(B - 1, tail_of("dve"))

        def h(n, c):
            cc = n * NC + c
            s = stage[:, 2 + c % 2]
            dve.wait_ge(silu_done, cc + 1)
            dve.wait_ge(cb_done, n * z.NQ + c // z.CQ + 1)
            nc.vector.tensor_tensor(s, s, ps[:, CB], ALU.mult).then_inc(sc_done, 1)
            dve.wait_ge(sc_done, cc + 1)
            dve.wait_ge(up_done, cc + 1)
            nc.vector.tensor_tensor(s, s, ps[:, UP], ALU.mult).then_inc(h_done, 1)

        def first(n, b):
            norm(n, b)
            x_lo(n)
            dve.wait_ge(const_in, 64)
            route_shift(n)
            route_first(n)
            route_second(n)
            route_weights()
            route_parts()

        def residual(n, b):
            dve.wait_ge(ffn_back, n + 1)
            xs = x[:, b].rearrange("p t d -> p (t d)") if type(b) is int else \
                x[:, bass.ds(b, 1)].rearrange("p a t d -> p (a t d)")
            nc.vector.tensor_tensor(xs, xs, ps[:, MISC:MISC + 2].rearrange("p a c -> p (a c)"), ALU.add).then_inc(x_done, 1)

        def bridge(c):
            if c == 2:
                for t in range(T):
                    norm_stats(0, t)
                mean_start()
                rsqrt_start()
            if c == 3:
                for _ in range(3):
                    rsqrt_step()
            if c == 4:
                normalise(0, 0, axn_done)
                normalise(0, 2, axn_done)
            if c == 8:
                for kk in range(K):
                    dve.wait_ge(bx_hi, kk + 1)
                    nc.vector.tensor_tensor(bx_at(kk, 1), xf[:, kk], bx_at(kk, 0).bitcast(F32), ALU.subtract).then_inc(bx_lo, 1)
            if c >= TASKS_FROM:
                r = c - TASKS_FROM
                if r == 0:
                    dve.wait_ge(tab_in, 32)
                task(0, -1, FIRST[r], counts=first_counts(r))
                if r > 0:
                    rope_lo(r - 1)

        def bridge_end(n, b):
            dve.wait_ge(up_done, (n + 1) * NC)
            for kk in range(K):
                nc.vector.tensor_copy(xl[:, kk], bx_at(kk, 1).bitcast(F32)).then_inc(ax_lo, 1)
            for r in range(NC - TASKS_FROM, G + 1):
                task(0, -1, FIRST[r], counts=first_counts(r))
                rope_lo(r - 1)
                if r == G:
                    residual(n, b)
            task(0, -1, VALUES, counts=first_counts(G + 2))
            rope_lo(G)

        def rope_lo(r):
            dve.wait_ge(q_hi, r + 1)
            hi, lo = (k_at(0, q) if FIRST[r] == KCOL else q_at(0, FIRST[r], q) for q in (0, 1))
            nc.vector.tensor_tensor(lo, xf[:, r % 2], hi.bitcast(F32), ALU.subtract).then_inc(q_lo, 1)

        def batch(turn, n, b, last, start=False):
            for c in range(2, NC):
                h(n, c)
                if last and turn == 0:
                    bridge(c)
                if last:
                    continue
                if start and c == 2:
                    dve.wait_ge(x_in[1], 16)
                if c == 2:
                    for t in range(T):
                        norm_stats(b + 1, t)
                    mean_start()
                    rsqrt_start()
                if c == 3:
                    for _ in range(3):
                        rsqrt_step()
                if c == 4:
                    normalise(b + 1, 0, xn_done)
                    normalise(b + 1, 2, xn_done)
                if c == 7:
                    route_shift(n + 1)
                if c == 8:
                    route_first(n + 1)
                if c == 9:
                    route_second(n + 1)
                if c == 10:
                    route_weights()
                    dve.wait_ge(combT_ps, n + 1)
                    route_parts()
            if not last:
                x_lo(n + 1)
                h(n + 1, 0)
                h(n + 1, 1)
            if last and turn == 0:
                bridge_end(n, b)
            else:
                residual(n, b)

        def ffn(n0):
            if n0 == 0:
                first(n0, 0)
                h(n0, 0)
            h(n0, 1)
            b0 = 0
            if n0 == 0:
                batch(0, 0, 0, False, start=True)
                for b in range(2, B):
                    dve.wait_ge(x_in[b], 16)
                b0 = 1
            per = chain["n"]
            with dve.Fori(b0, B - 1) as b:
                chain["loop"] = b * PER
                chain["n"] = per - b0 * PER
                batch(n0 // B, b + n0, b, False)
            chain["n"] = per + (B - 1 - b0) * PER
            chain["loop"] = 0
            batch(n0 // B, n0 + B - 1, B - 1, True)

        PER = T + 9 + 9 + 1 + 6 + 5 + 9

        nc.vector.memset(comb[:], 0.0).then_inc(comb_zero, 1)
        dve.wait_ge(comb_zero, 1)
        dve.wait_ge(x_in[0], 16)
        ffn(0)
        attention()
        ffn(B)

    @block.gpsimd
    def _(pool):
        def h_lo(n, c):
            cc = n * NC + c
            pool.wait_ge(hi_done, cc + 1)
            if not (type(n) is int and cc < 2):
                pool.wait_ge(down_done, cc - 1)
            nc.gpsimd.tensor_tensor(hl[:, c % 2], stage[:, 2 + c % 2], hh[:, c % 2].bitcast(F32), ALU.subtract)\
              .then_inc(lo_done, 1)

        def batch(turn, n, last, start=False):
            for c in range(2, NC):
                h_lo(n, c)
                if turn == 0 and not start and c - 2 < (attn_units(n) if last else AU):
                    attn_w_lo(n, c - 2)
                if start:
                    for p in SPLIT_AT.get(c, []):
                        weights_lo(p)
                if turn == 0 and last and c >= TASKS_FROM:
                    pool.wait_ge(tab_in, 32)
                    rope(0, -1, FIRST[c - TASKS_FROM], counts=first_counts(c - TASKS_FROM))
            if not last:
                h_lo(n + 1, 0)
                h_lo(n + 1, 1)

        def attn_w_lo(b, j):
            pool.wait_ge(w_hi, b * AU + z.UF - AU + j + 1)
            nc.gpsimd.tensor_tensor(attn_w(b, j, 1), stage[:, j % 2], attn_w(b, j, 0).bitcast(F32), ALU.subtract)\
              .then_inc(w_lo, 1)

        def ffn(n0):
            if n0 == 0:
                weights_lo(4)
            h_lo(n0, 0)
            if n0 == 0:
                weights_lo(5)
            h_lo(n0, 1)
            if n0 == 0:
                weights_lo(6)
                batch(0, 0, False, start=True)
            with pool.Fori(n0 or 1, n0 + B - 1) as n:
                batch(n0 // B, n, False)
            batch(n0 // B, n0 + B - 1, True)

        def weights_lo(p):
            hi, lo = (ffn_w(0, BY_USE[p], part) for part in (0, 1))
            pool.wait_ge(w_hi, p + 1)
            nc.gpsimd.tensor_tensor(lo, stage[:, stage_slot(p)], hi.bitcast(F32), ALU.subtract).then_inc(w_lo, 1)

        def reload_lo(u):
            pool.wait_ge(w_hi, SPLIT + u + 1)
            nc.gpsimd.tensor_tensor(ffn_w(1, u, 1), reload_slot(u), ffn_w(1, u, 0).bitcast(F32), ALU.subtract).then_inc(w_lo, 1)

        def rope(b, k, col, counts=None):
            if col < 0 or col == VCOL:
                return
            c = counts or [JB[i] * b + v for i, v in enumerate(task_count(k, col))]
            g = k // T + 1
            pool.wait_ge(proj_act, c[0] + 1)
            slot = rope_slot(col)
            nc.gpsimd.tensor_tensor(ropeB[:, slot], ropeB[:, slot], sin[:], ALU.mult).then_inc(rope_mul, 1)
            pool.wait_ge(rope_mul, c[1] + 1)
            pool.wait_ge(proj_dve, c[2] + 1)
            nc.gpsimd.tensor_tensor(xf[:, slot], xf[:, slot], ropeB[:, slot], ALU.add).then_inc(rope_sum, 1)

        def rope_lo(b, k, col, counts=None):
            c = counts or [JB[i] * b + v for i, v in enumerate(task_count(k, col))]
            g = k // T + 1
            pool.wait_ge(q_hi, c[1] + 1)
            hi, lo = (k_at(g, q) if col == KCOL else q_at(g, col, q) for q in (0, 1))
            nc.gpsimd.tensor_tensor(lo, xf[:, rope_slot(col)], hi.bitcast(F32), ALU.subtract).then_inc(q_lo, 1)

        def do(b, items):
            for what, k, n in items:
                if what == "PM":
                    rope(b, k, n)
                elif what == "PL":
                    rope_lo(b, k, n)
                else:
                    reload_lo(n)

        for p in range(4):
            weights_lo(p)
        ffn(0)
        for r in range(NC - TASKS_FROM, G + 1):
            rope(0, -1, FIRST[r], counts=first_counts(r))
        do(0, head_of("pool"))
        with pool.Fori(0, B - 1) as b:
            do(b, turn_of("pool"))
        do(B - 1, tail_of("pool"))
        ffn(B)

    @block.tensor
    def _(pe):
        def mm(out, lhsT, rhs, start, stop, **kw):
            return nc.tensor.matmul(out, lhsT, rhs, start=start, stop=stop, **kw)

        def transposes(n):
            for t in range(T):
                if t % 2 == 0:
                    pe.wait_ge(xn_done, 2 * n + 1 + t // 2)
                for k in range(K):
                    ins = nc.tensor.transpose(ps[:, MISC + k, t * P:(t + 1) * P],
                                              work[:, t * D + k * P:t * D + (k + 1) * P], ident[:])
            ins.then_inc(xnT_done, 1)

        def route(n):
            if not (type(n) is int and n % B == 0):
                pe.wait_ge(combT_done, n)
            pe.wait_ge(xf_done, n + 1)
            for t in range(T):
                for k in range(K):
                    ins = mm(ps[:, LOG, t * E:(t + 1) * E], xf[:, k, t * P:(t + 1) * P], router[:, k], k == 0, k == K - 1)
            ins.then_inc(logit_done, 1)

        def comb_transposes(n):
            pe.wait_ge(comb_done, n + 1)
            for t in range(T):
                ins = nc.tensor.transpose(ps[:, LOG].bitcast(BF16)[:, t * P:(t + 1) * P], comb[:, t], identb[:])
            ins.then_inc(combT_ps, 1)

        def gate_up(wt, n, c):
            cc = n * NC + c
            if type(n) is int and n == 0:
                pe.wait_ge(w_lo, BY_USE.index(c) + 1)
            for which, bank, free, done in ((0, GATE, silu_done, gate_done), (1, UP, h_done, up_done)):
                if not (type(n) is int and cc == 0):
                    pe.wait_ge(free, cc)
                o = ps[:, bank]
                for k in range(K):
                    if c == 0:
                        pe.wait_ge(xh_done, K * n + k + 1)
                    mm(o, gu_w(wt, c, which, k, 0), xh[:, k], k == 0, False)
                    mm(o, gu_w(wt, c, which, k, 1), xh[:, k], False, False)
                for k in range(K):
                    if c == 0:
                        pe.wait_ge(xl_done, K * n + k + 1)
                    ins = mm(o, gu_w(wt, c, which, k, 0), xl[:, k], False, k == K - 1)
                ins.then_inc(done, 1)

        def combine(n, c):
            if c % z.CQ == 0:
                if not (type(n) is int and n * NC + c == 0):
                    pe.wait_ge(sc_done, n * NC + c)
                if c == 0:
                    pe.wait_ge(combT_done, n + 1)
                q = c // z.CQ
                mm(ps[:, CB], expand[:, q * P:(q + 1) * P], combT[:], True, True).then_inc(cb_done, 1)

        def down(wt, base, n, c):
            cc = n * NC + c
            if type(n) is int and n == 0:
                pe.wait_ge(w_lo, BY_USE.index(z.UG + c // 2) + 1)
            pe.wait_ge(lo_done, cc + 1)
            for k in range(K):
                o = ps[:, DOWN + k]
                mm(o, down_w(wt, base, c, k, 0), hh[:, c % 2], c == 0, False)
                mm(o, down_w(wt, base, c, k, 1), hh[:, c % 2], False, False)
                ins = mm(o, down_w(wt, base, c, k, 0), hl[:, c % 2], False, c == NC - 1)
            ins.then_inc(down_done, 1)

        def back(n):
            pe.wait_ge(ffn_evac, n + 1)
            for t in range(T):
                for k in range(K):
                    at = (t % 2) * D + k * P
                    ins = nc.tensor.transpose(ps[:, MISC + t // 2, at:at + P], work[:, k * S + t * P:k * S + (t + 1) * P],
                                              ident[:])
            ins.then_inc(ffn_back, 1)

        def batch(wt, wd, base, n, last):
            to_attention = last and n == B - 1
            for c in range(2, NC):
                gate_up(wt, n, c)
                combine(n, c)
                if to_attention and c >= TASKS_FROM:
                    first_task(c - TASKS_FROM)
                if c == NC - 1 and not last:
                    comb_transposes(n + 1)
                down(wd, base, n, c - 1)
                if c == 5 and not last:
                    transposes(n + 1)
                if c == 5 and to_attention:
                    pe.wait_ge(axn_done, 2)
                    for kk in range(K):
                        for t in range(T):
                            ins = nc.tensor.transpose(ps[:, MISC + kk, t * P:(t + 1) * P],
                                                      work[:, t * D + kk * P:t * D + (kk + 1) * P], ident[:])
                    ins.then_inc(bxT_done, 1)
                if not last and c == 7:
                    route(n + 1)
            if to_attention:
                first_task(NC - TASKS_FROM)
            if last:
                down(wd, base, n, NC - 1)
                if to_attention:
                    first_task(G)
                    pe.wait_ge(proj_act, G)
                    pe.wait_ge(proj_dve, G)
                back(n)
                return
            gate_up(wt, n + 1, 0)
            combine(n + 1, 0)
            down(wd, base, n, NC - 1)
            gate_up(wt, n + 1, 1)
            combine(n + 1, 1)
            back(n)
            down(wd, base, n + 1, 0)

        def ffn(wt, wd, base, n0):
            if n0 == 0:
                transposes(n0)
                pe.wait_ge(router_in, 16)
                route(n0)
            if n0 == 0:
                gate_up(wt, n0, 0)
                pe.wait_ge(const_in, 64)
                comb_transposes(n0)
                combine(n0, 0)
            gate_up(wt, n0, 1)
            combine(n0, 1)
            down(wd, base, n0, 0)
            if n0 == 0:
                batch(wt, wd, base, n0, False)
            with pe.Fori(n0 or 1, n0 + B - 1) as n:
                batch(wt, wd, base, n, False)
            batch(wt, wd, base, n0 + B - 1, True)

        def bank_free(k, c):
            if k >= 0:
                pe.wait_ge(proj_act, c[0])
                pe.wait_ge(proj_dve, c[2])
            elif c[0] == 0:
                pe.wait_ge(combT_done, B)
            elif c[0] == 1:
                pe.wait_ge(bxf_done, 1)
            elif c[0] == G + 1:
                pe.wait_ge(sc_done, B * NC)
            else:
                pe.wait_ge(proj_act, c[0] - 1)
                pe.wait_ge(proj_dve, min(c[0] - 1, G + 1))

        def ax_transposes(b, kk, c):
            last = type(b) is int and b == B
            pe.wait_ge(xn_done if last else axn_done, 2 * b + 2)
            pe.wait_ge(proj_act, c[0])
            pe.wait_ge(proj_dve, c[2] - kk if last else c[2])
            for t in range(T):
                ins = nc.tensor.transpose(ps[:, JBANK, t * P:(t + 1) * P], work[:, t * D + kk * P:t * D + (kk + 1) * P], ident[:])
            ins.then_inc(xnT_done if last and kk == K - 1 else proj_done, 1)

        def first_task(r):
            if r == 0:
                pe.wait_ge(w_lo, z.UF + z.UA)
                pe.wait_ge(bx_lo, K)
            task(0, -1, FIRST[r], counts=first_counts(r))

        def task(b, k, col, counts=None):
            c = counts or [JB[i] * b + v for i, v in enumerate(task_count(k, col))]
            if col < 0:
                return ax_transposes(b + 1, -1 - col, c)
            bank_free(k, c)
            bank = bank_of_task(k, c)
            g = (k // T + 1) % KV
            if k >= 0 and type(b) is int and b == 0:
                pe.wait_ge(ax_hi, K)
                pe.wait_ge(ax_lo, K)
            xh_k, xl_k = ((lambda kk: xh[:, kk], lambda kk: xl[:, kk]) if k >= 0 else
                          (lambda kk: bx_at(kk, 0), lambda kk: bx_at(kk, 1)))
            if col == VALUES:
                pe.wait_ge(proj_act, c[0])
                for t in range(T):
                    ins = nc.tensor.transpose(ps[:, bank, t * P:(t + 1) * P], ropeB[:, rope_slot(VCOL), t * P:(t + 1) * P],
                                              ident[:])
            else:
                o = ps[:, bank]
                for kk in range(K):
                    mm(o, qkv_w(g, col, kk, 0), xh_k(kk), kk == 0, False)
                    mm(o, qkv_w(g, col, kk, 1), xh_k(kk), False, False)
                    ins = mm(o, qkv_w(g, col, kk, 0), xl_k(kk), False, kk == K - 1)
            ins.then_inc(proj_done, 1)

        def scores_of(b, k, h):
            g, i = divmod(k, T)
            m = k * G + h
            if not (type(b) is int and b == 0 and m < 3):
                pe.wait_ge(exp_done, b * UB * G + m - bank_before(m) + 1)
            elif m == 0:
                pe.wait_ge(h_done, B * NC)
            elif bank_of(m) == CB:
                pe.wait_ge(proj_act, G + 2)
            if h == 0 and i == 0:
                pe.wait_ge(q_lo, (G + 1) * (KV * b + g) + 1)
            if i == 0:
                pe.wait_ge(q_lo, (G + 1) * (KV * b + g) + 2 + h)
            o = ps[:, bank_of(m % (UB * G)), 0:(i + 1) * P]
            rows = slice(i * P, (i + 1) * P)
            mm(o, q_at(g, h, 0)[:, rows], k_at(g, 0)[:, 0:(i + 1) * P], True, False)
            mm(o, q_at(g, h, 0)[:, rows], k_at(g, 1)[:, 0:(i + 1) * P], False, False)
            mm(o, q_at(g, h, 1)[:, rows], k_at(g, 0)[:, 0:(i + 1) * P], False, False)
            mm(o[:, rows], identb[:], causal[:], False, True).then_inc(s_done, 1)

        def prob_transposes(b, k, j):
            tb = tiles_before(k) + j
            if not (type(b) is int and b == 0 and tb < 2):
                pe.wait_ge(pt_lo, b * PB + tb - 1)
            for h in range(G):
                if j == 0:
                    pe.wait_ge(exp_done, b * UB * G + k * G + h + 1)
                ins = nc.tensor.transpose(ps[:, TBANK + tb % 2, h * P:(h + 1) * P], prob[k % 2][:, h, j * P:(j + 1) * P],
                                          ident[:])
            ins.then_inc(pt_done, 1)

        def values_of(b, k, j):
            g, i = divmod(k, T)
            tb = tiles_before(k) + j
            pe.wait_ge(pt_lo, b * PB + tb + 1)
            if j == 0:
                if not (type(b) is int and b == 0 and k == 0):
                    pe.wait_ge(a_lo, b * UB + k)
                else:
                    pe.wait_ge(x_done, B)
                if i == 0:
                    pe.wait_ge(proj_dve, JB[2] * b + values_use(g))
            keys = slice(j * P, (j + 1) * P)
            o = ps[:, OBANK]
            mm(o, v_at(g, 0)[:, keys], pT_at(tb, 0), j == 0, False)
            mm(o, v_at(g, 1)[:, keys], pT_at(tb, 0), False, False)
            mm(o, v_at(g, 0)[:, keys], pT_at(tb, 1), False, j == i).then_inc(pv_done, 1)

        def project(b, k, half):
            g = (k // T) % KV
            pe.wait_ge(a_lo, b * UB + k + 1)
            if not (type(b) is int and b == 0 and k == 0 and half == 0):
                pe.wait_ge(xadd_done, G * (b * UB + k) + 2 * half)
            for h in (2 * half, 2 * half + 1):
                o = ps[:, WBANK, (h % 2) * D:(h % 2) * D + D]
                rows = slice(h * P, (h + 1) * P)
                mm(o, a_at(k, 0)[:, rows], wo_w(g, h, 0), True, False)
                mm(o, a_at(k, 0)[:, rows], wo_w(g, h, 1), False, False)
                ins = mm(o, a_at(k, 1)[:, rows], wo_w(g, h, 0), False, True)
            ins.then_inc(wo_done, 1)

        def do(b, items):
            for what, k, n in items:
                if what == "S":
                    scores_of(b, k, n)
                elif what == "T":
                    prob_transposes(b, k, n)
                elif what == "V":
                    values_of(b, k, n)
                elif what == "W":
                    project(b, k, n)
                elif what == "J":
                    task(b, k, n)
                elif what == "route":
                    route(B)
                elif what == "comb_T":
                    comb_transposes(B)
                elif what == "gates":
                    pe.wait_ge(w_lo, SPLIT + 1)
                    pe.wait_ge(exp_done, B * UB * G)
                    gate_up(wA, B, 0)
                else:
                    pe.wait_ge(refill, 16)
                    combine(B, 0)

        pe.wait_ge(ident_in, 16)
        ffn(wF, wF, z.UG, 0)
        for r in (G + 1, G + 2):
            first_task(r)
        do(0, head_of("pe"))
        with pe.Fori(0, B - 1) as b:
            do(b, turn_of("pe"))
        do(B - 1, tail_of("pe"))
        pe.wait_ge(w_lo, SPLIT + z.UF)
        pe.wait_ge(pt_lo, B * PB)
        ffn(wA, wF, 0, B)


def layouts(L0_attn_x, L0_attn_Wqkv, L0_attn_Wo, L0_ffn_router_w, L0_ffn_gate_w, L0_ffn_up_w, L0_ffn_down_w):
    f = np.float32
    x, wqkv, wo, rw, gw, uw, dw = (np.asarray(a) for a in (
        L0_attn_x, L0_attn_Wqkv, L0_attn_Wo, L0_ffn_router_w, L0_ffn_gate_w, L0_ffn_up_w, L0_ffn_down_w))
    z = Sizes(x.shape, wqkv.shape, wo.shape, rw.shape, gw.shape)
    B, S, D, T, K, H, KV, G = z.B, z.S, z.D, z.T, z.K, z.H, z.KV, z.G
    def chunks(w):
        w = w.reshape(z.NQ, z.QE, z.CQ, z.FC, D).transpose(0, 2, 1, 3, 4)
        return w.reshape(z.EF, D)

    gu = [chunks(w.transpose(0, 2, 1)).T.reshape(K, P, z.NC, P).transpose(2, 1, 0, 3) for w in (gw, uw)]
    gu = np.concatenate(gu, axis=2).reshape(z.UG, P, 512)
    dn = chunks(dw).reshape(z.UD, 2, P, D).transpose(0, 2, 1, 3).reshape(z.UD, P, 512)
    w = wqkv.reshape(K, P, H + 2 * KV, P)
    heads = [j for g in range(KV) for j in [*range(G * g, G * g + G), H + g, H + KV + g]]
    qkv = w[:, :, heads].reshape(K, P, z.UQ, 2, P).transpose(2, 1, 3, 0, 4).reshape(z.UQ, P, 512)
    won = wo.reshape(z.UO, 2, P, D).transpose(0, 2, 1, 3).reshape(z.UO, P, 512)
    half = P // 2
    freqs = (f(1.0) / f(10000.0) ** (np.arange(0, P, 2, dtype=f) / f(P))).astype(f)
    ang = np.arange(S, dtype=f)[None, :] * freqs[:, None]
    expand = np.zeros((P, z.E * z.FC), f)
    for r in range(3 * z.E):
        e = r % z.E
        expand[r, e * z.FC:(e + 1) * z.FC] = 1
    return z, {
        "x": np.ascontiguousarray(x.reshape(B, T, P, D).transpose(0, 2, 1, 3)),
        "wffn": np.ascontiguousarray(np.concatenate([gu, dn])),
        "wattn": np.ascontiguousarray(np.concatenate([qkv, won])),
        "router": np.ascontiguousarray(rw.reshape(K, P, z.E).transpose(1, 0, 2)),
        "revidx": np.tile(np.arange(z.E, 0, -1, dtype=f), (P, 1)),
        "ident": np.eye(P, dtype=f),
        "identb": np.eye(P, dtype=f).astype(np.dtype("bfloat16")),
        "expand": expand.astype(np.dtype("bfloat16")),
        "causal": np.triu(np.full((P, P), -2.3819763e38, f), k=1).astype(np.dtype("bfloat16")),
        "cos": np.concatenate([np.cos(ang), np.cos(ang)]).astype(f),
        "sin": np.concatenate([-np.sin(ang), np.sin(ang)]).astype(f),
    }


def kernel(**inputs):
    import concourse.bacc as bacc
    from concourse.bass_utils import run_bass_kernel_spmd

    z, arrays = layouts(**inputs)
    arrays = {f"in_{name}": a for name, a in arrays.items()}
    nc = bacc.Bacc("TRN2", target_bir_lowering=False, num_devices=1)
    dram = {name[3:]: nc.dram_tensor(name, a.shape, mybir.dt.from_np(a.dtype), kind="ExternalInput").ap()
            for name, a in arrays.items()}
    dram["out"] = nc.dram_tensor("out_y", (z.B, P, z.T, z.D), F32, kind="ExternalOutput").ap()
    build(nc, dram, z)
    y = run_bass_kernel_spmd(nc, [arrays], core_ids=[0]).results[0]["out_y"]
    return y.transpose(0, 2, 1, 3).reshape(z.B, z.S, z.D)
```
